# Optimizing a Trainium2 kernel written in Bass

```python
import numpy as np
import jax
import jax.numpy as jnp

def _softmax(x, axis=-1):
    return jax.nn.softmax(x, axis=axis)

def _gelu(x):
    return jax.nn.gelu(x, approximate=True)

def _silu(x):
    return jax.nn.silu(x)

def _sigmoid(x):
    return jax.nn.sigmoid(x)

def _layernorm(x, axis=-1, eps=1e-05):
    m = jnp.mean(x, axis=axis, keepdims=True)
    v = jnp.var(x, axis=axis, keepdims=True)
    return (x - m) / jnp.sqrt(v + eps)

def _scatter_add(tgt, idx, src, axis=0):
    return tgt.at[idx].add(src)

def _segment_sum(src, seg, n):
    return jax.ops.segment_sum(src, seg, n)
kernel_name = 'mk_decoder_preln_d1_seqx_r8_e9571b'

def setup_inputs(seed: int=0):
    np.random.seed(seed)
    _w = jnp.asarray

    def _rec_inputs():
        import jax
        import jax.numpy as jnp
        _rk = jax.random.key(seed)
        x = -0.0003929 + 0.9999 * jax.random.normal(jax.random.fold_in(_rk, 1), (16, 64, 128), jnp.float32)
        _lenS = 64 - jax.random.randint(jax.random.fold_in(_rk, 7), (16,), 0, max(1, 64 // 4) + 1, jnp.int32)
        _lenS2 = 64 - jax.random.randint(jax.random.fold_in(_rk, 8), (16,), 0, max(1, 64 // 4) + 1, jnp.int32)
        _ctx_768P = jax.random.normal(jax.random.fold_in(_rk, 11), (16, 16, 96), jnp.float32)
        _ctx_768c = jax.random.dirichlet(jax.random.fold_in(_rk, 511), 0.3 * jnp.ones((16,), jnp.float32), (16, 64))
        _ctx_768t = jnp.einsum('bsk,bkd->bsd', _ctx_768c, _ctx_768P)
        _ctx_768t = _ctx_768t * jax.lax.rsqrt(jnp.mean(jnp.square(_ctx_768t)) + 1e-12) * 0.953939
        ctx_768 = 2.09791e-05 + 1.00001 * (_ctx_768t + 0.3 * jax.random.normal(jax.random.fold_in(_rk, 611), (16, 64, 96), jnp.float32))
        return (x, ctx_768)
    x, ctx_768 = _rec_inputs()

    def _L0_attn_setup():
        import jax, jax.numpy as jnp
        import numpy as np
        HIDDEN = 128
        HEADS = 16
        HEAD_DIM = HIDDEN // HEADS
        ROPE_BASE = 10000.0

        def _rope_cos_sin(seq_len, dim):
            inv_freq = 1.0 / ROPE_BASE ** (jnp.arange(0, dim, 2, dtype=jnp.float32) / dim)
            t = jnp.arange(seq_len, dtype=jnp.float32)
            freqs = jnp.einsum('i,j->ij', t, inv_freq)
            emb = jnp.concatenate([freqs, freqs], axis=-1)
            return (jnp.cos(emb), jnp.sin(emb))

        def _apply_rope(x, cos, sin):
            x1, x2 = (x[..., 0::2], x[..., 1::2])
            c = cos[..., :x1.shape[-1]]
            s = sin[..., :x1.shape[-1]]
            return jnp.concatenate([x1 * c - x2 * s, x1 * s + x2 * c], axis=-1)
        key = jax.random.key(seed)
        ks = jax.random.split(key, 9)
        B, S = (4, 256)
        lim = 1.0 / np.sqrt(HIDDEN)

        def lin(kw, kb):
            W = jax.random.uniform(kw, (HIDDEN, HIDDEN), jnp.float32, -lim, lim)
            b = jax.random.uniform(kb, (HIDDEN,), jnp.float32, -lim, lim)
            return (W, b)
        Wq, bq = lin(ks[0], ks[1])
        Wk, bk = lin(ks[2], ks[3])
        Wv, bv = lin(ks[4], ks[5])
        Wo, bo = lin(ks[6], ks[7])
        x = jax.random.normal(ks[8], (B, S, HIDDEN), jnp.float32)
        return {'x': x, 'Wq': Wq, 'bq': bq, 'Wk': Wk, 'bk': bk, 'Wv': Wv, 'bv': bv, 'Wo': Wo, 'bo': bo}
    _L0_attn_all = _L0_attn_setup()
    _L0_attn_in = {k: v for k, v in _L0_attn_all.items() if k in ('Wq', 'bq', 'Wk', 'bk', 'Wv', 'bv', 'Wo', 'bo')}
    del _L0_attn_all

    def _L0_xattn_setup():
        import jax, jax.numpy as jnp
        import numpy as np
        HEADS = 8
        DIM_HEAD = 64
        QUERY_DIM = 128
        CONTEXT_DIM = 96
        INNER = HEADS * DIM_HEAD
        key = jax.random.key(seed)
        ks = jax.random.split(key, 7)
        B, Sq, Skv = (4, 512, 128)
        x = jax.random.normal(ks[0], (B, Sq, QUERY_DIM), dtype=jnp.float32)
        context = jax.random.normal(ks[1], (B, Skv, CONTEXT_DIM), dtype=jnp.float32)
        Wq = jax.random.normal(ks[2], (QUERY_DIM, INNER), dtype=jnp.float32) * QUERY_DIM ** (-0.5)
        Wk = jax.random.normal(ks[3], (CONTEXT_DIM, INNER), dtype=jnp.float32) * CONTEXT_DIM ** (-0.5)
        Wv = jax.random.normal(ks[4], (CONTEXT_DIM, INNER), dtype=jnp.float32) * CONTEXT_DIM ** (-0.5)
        Wo = jax.random.normal(ks[5], (INNER, QUERY_DIM), dtype=jnp.float32) * INNER ** (-0.5)
        bo = jax.random.normal(ks[6], (QUERY_DIM,), dtype=jnp.float32) * 0.01
        return {'x': x, 'context': context, 'Wq': Wq, 'Wk': Wk, 'Wv': Wv, 'Wo': Wo, 'bo': bo}
    _L0_xattn_all = _L0_xattn_setup()
    _L0_xattn_in = {k: v for k, v in _L0_xattn_all.items() if k in ('Wq', 'Wk', 'Wv', 'Wo', 'bo')}
    del _L0_xattn_all

    def _L0_ffn_setup():
        import jax, jax.numpy as jnp
        import numpy as np
        B, L, D = (4, 256, 128)
        E, K, S = (8, 2, 2)
        F = 176
        SCALE = 1.0
        INIT = 0.02

        def _swiglu(x, wg, wu, wd):
            return jax.nn.silu(x @ wg) * (x @ wu) @ wd
        key = jax.random.key(seed)
        ks = jax.random.split(key, 8)
        return {'hidden_states': jax.random.normal(ks[0], (B, L, D), jnp.float32), 'gate_w': jax.random.normal(ks[1], (D, E), jnp.float32) * INIT, 'exp_gate': jax.random.normal(ks[2], (E, D, F), jnp.float32) * INIT, 'exp_up': jax.random.normal(ks[3], (E, D, F), jnp.float32) * INIT, 'exp_down': jax.random.normal(ks[4], (E, F, D), jnp.float32) * INIT, 'sh_gate': jax.random.normal(ks[5], (S, D, F), jnp.float32) * INIT, 'sh_up': jax.random.normal(ks[6], (S, D, F), jnp.float32) * INIT, 'sh_down': jax.random.normal(ks[7], (S, F, D), jnp.float32) * INIT}
    _L0_ffn_all = _L0_ffn_setup()
    _L0_ffn_in = {k: v for k, v in _L0_ffn_all.items() if k in ('gate_w', 'exp_gate', 'exp_up', 'exp_down', 'sh_gate', 'sh_up', 'sh_down')}
    del _L0_ffn_all
    return {'x': x, 'ctx_768': ctx_768, 'L0_attn_Wq': _L0_attn_in['Wq'], 'L0_attn_bq': _L0_attn_in['bq'], 'L0_attn_Wk': _L0_attn_in['Wk'], 'L0_attn_bk': _L0_attn_in['bk'], 'L0_attn_Wv': _L0_attn_in['Wv'], 'L0_attn_bv': _L0_attn_in['bv'], 'L0_attn_Wo': _L0_attn_in['Wo'], 'L0_attn_bo': _L0_attn_in['bo'], 'L0_xattn_Wq': _L0_xattn_in['Wq'], 'L0_xattn_Wk': _L0_xattn_in['Wk'], 'L0_xattn_Wv': _L0_xattn_in['Wv'], 'L0_xattn_Wo': _L0_xattn_in['Wo'], 'L0_xattn_bo': _L0_xattn_in['bo'], 'L0_ffn_gate_w': _L0_ffn_in['gate_w'], 'L0_ffn_exp_gate': _L0_ffn_in['exp_gate'], 'L0_ffn_exp_up': _L0_ffn_in['exp_up'], 'L0_ffn_exp_down': _L0_ffn_in['exp_down'], 'L0_ffn_sh_gate': _L0_ffn_in['sh_gate'], 'L0_ffn_sh_up': _L0_ffn_in['sh_up'], 'L0_ffn_sh_down': _L0_ffn_in['sh_down']}

def reference(x, ctx_768, L0_attn_Wq, L0_attn_bq, L0_attn_Wk, L0_attn_bk, L0_attn_Wv, L0_attn_bv, L0_attn_Wo, L0_attn_bo, L0_xattn_Wq, L0_xattn_Wk, L0_xattn_Wv, L0_xattn_Wo, L0_xattn_bo, L0_ffn_gate_w, L0_ffn_exp_gate, L0_ffn_exp_up, L0_ffn_exp_down, L0_ffn_sh_gate, L0_ffn_sh_up, L0_ffn_sh_down):
    import jax
    import jax.numpy as jnp

    def _L0_attn_ref(x, Wq, bq, Wk, bk, Wv, bv, Wo, bo):
        import jax, jax.numpy as jnp
        import numpy as np
        HIDDEN = 128
        HEADS = 16
        HEAD_DIM = HIDDEN // HEADS
        ROPE_BASE = 10000.0

        def _rope_cos_sin(seq_len, dim):
            inv_freq = 1.0 / ROPE_BASE ** (jnp.arange(0, dim, 2, dtype=jnp.float32) / dim)
            t = jnp.arange(seq_len, dtype=jnp.float32)
            freqs = jnp.einsum('i,j->ij', t, inv_freq)
            emb = jnp.concatenate([freqs, freqs], axis=-1)
            return (jnp.cos(emb), jnp.sin(emb))

        def _apply_rope(x, cos, sin):
            x1, x2 = (x[..., 0::2], x[..., 1::2])
            c = cos[..., :x1.shape[-1]]
            s = sin[..., :x1.shape[-1]]
            return jnp.concatenate([x1 * c - x2 * s, x1 * s + x2 * c], axis=-1)
        B, S, _ = x.shape
        scale = HEAD_DIM ** (-0.5)

        def proj(W, b):
            y = jnp.einsum('bsd,ed->bse', x, W) + b
            return y.reshape(B, S, HEADS, HEAD_DIM).transpose(0, 2, 1, 3)
        q = proj(Wq, bq)
        k = proj(Wk, bk)
        v = proj(Wv, bv)
        cos, sin = _rope_cos_sin(S, HEAD_DIM)
        cos = cos[None, None]
        sin = sin[None, None]
        q = _apply_rope(q, cos, sin) * scale
        k = _apply_rope(k, cos, sin)
        attn = jnp.einsum('bhsd,bhtd->bhst', q, k)
        attn = jax.nn.softmax(attn, axis=-1)
        out = jnp.einsum('bhst,bhtd->bhsd', attn, v)
        out = out.transpose(0, 2, 1, 3).reshape(B, S, HIDDEN)
        return jnp.einsum('bsd,ed->bse', out, Wo) + bo

    def _L0_xattn_ref(x, context, Wq, Wk, Wv, Wo, bo):
        import jax, jax.numpy as jnp
        import numpy as np
        HEADS = 8
        DIM_HEAD = 64
        QUERY_DIM = 128
        CONTEXT_DIM = 96
        INNER = HEADS * DIM_HEAD
        B, Sq, _ = x.shape
        h, d = (HEADS, DIM_HEAD)
        scale = d ** (-0.5)
        q = (x @ Wq).reshape(B, Sq, h, d).transpose(0, 2, 1, 3)
        k = (context @ Wk).reshape(B, -1, h, d).transpose(0, 2, 1, 3)
        v = (context @ Wv).reshape(B, -1, h, d).transpose(0, 2, 1, 3)
        scores = jnp.einsum('bhid,bhjd->bhij', q, k) * scale
        attn = jax.nn.softmax(scores, axis=-1)
        out = jnp.einsum('bhij,bhjd->bhid', attn, v)
        out = out.transpose(0, 2, 1, 3).reshape(B, Sq, h * d)
        return out @ Wo + bo

    def _L0_ffn_ref(hidden_states, gate_w, exp_gate, exp_up, exp_down, sh_gate, sh_up, sh_down):
        import jax, jax.numpy as jnp
        import numpy as np
        B, L, D = (4, 256, 128)
        E, K, S = (8, 2, 2)
        F = 176
        SCALE = 1.0
        INIT = 0.02

        def _swiglu(x, wg, wu, wd):
            return jax.nn.silu(x @ wg) * (x @ wu) @ wd
        Bx, Lx, Dx = hidden_states.shape
        x = hidden_states.reshape(-1, Dx)
        T = x.shape[0]
        shared = jnp.zeros_like(x)
        for i in range(sh_gate.shape[0]):
            shared = shared + _swiglu(x, sh_gate[i], sh_up[i], sh_down[i])
        logits = x @ gate_w
        probs = jax.nn.softmax(logits.astype(jnp.float32), axis=-1)
        w, sel = jax.lax.top_k(probs, K)
        w = w / jnp.sum(w, axis=-1, keepdims=True)
        w = w.astype(hidden_states.dtype)
        Wte = jnp.zeros((T, exp_gate.shape[0]), hidden_states.dtype)
        Wte = Wte.at[jnp.arange(T)[:, None], sel].add(w)
        routed = jnp.zeros_like(x)
        for e in range(exp_gate.shape[0]):
            routed = routed + Wte[:, e:e + 1] * _swiglu(x, exp_gate[e], exp_up[e], exp_down[e])
        out = shared + SCALE * routed
        return out.reshape(Bx, Lx, Dx)
    x = x + _L0_attn_ref(_layernorm(x, axis=-1), L0_attn_Wq, L0_attn_bq, L0_attn_Wk, L0_attn_bk, L0_attn_Wv, L0_attn_bv, L0_attn_Wo, L0_attn_bo)
    x = x + _L0_xattn_ref(_layernorm(x, axis=-1), ctx_768, L0_xattn_Wq, L0_xattn_Wk, L0_xattn_Wv, L0_xattn_Wo, L0_xattn_bo)
    x = x + _L0_ffn_ref(_layernorm(x, axis=-1), L0_ffn_gate_w, L0_ffn_exp_gate, L0_ffn_exp_up, L0_ffn_exp_down, L0_ffn_sh_gate, L0_ffn_sh_up, L0_ffn_sh_down)
    return x

_drawn_inputs = setup_inputs


def setup_inputs(seed=0):
    import zlib

    import numpy as np

    out = dict(_drawn_inputs(seed))
    spreads = {}
    factors = {'L0_attn_Wq': 4.032,
     'L0_attn_bq': 8.0,
     'L0_attn_Wk': 3.958,
     'L0_attn_bk': 8.0,
     'L0_xattn_bo': 6.099,
     'L0_ffn_gate_w': 8.0,
     'L0_ffn_exp_gate': 8.0,
     'L0_ffn_exp_up': 8.0,
     'L0_ffn_exp_down': 8.0,
     'L0_ffn_sh_gate': 6.754,
     'L0_ffn_sh_up': 6.695,
     'L0_ffn_sh_down': 6.7}
    for name, (base, spread) in spreads.items():
        noise = np.random.default_rng([zlib.crc32(name.encode()), seed]).standard_normal(out[name].shape)
        drawn = base * np.exp(spread * noise) if base else spread * noise
        out[name] = jnp.asarray(drawn.astype(out[name].dtype))
    for name, factor in factors.items():
        out[name] = (out[name] * factor).astype(out[name].dtype)
    return out
```

```python
from contextlib import ExitStack

import numpy as np
import concourse.bass as bass
from concourse import mybir

P = 128
B, S, D = 16, 64, 128
T = B * S
NT = T // P
HALF = T // 2
TPH = NT // 2
BPH = B // 2
H1, D1 = 16, 8
G, HG = 4, 4
H2, D2 = 8, 64
HP = H2 // 2
DC = 96
E, F, NSH = 8, 176, 2
FT = (E + NSH) * F
KT = -(-FT // P)
RT = E * F // P
assert RT * P == E * F
EPS = 1e-5
SCALE1, SCALE2 = D1 ** -0.5, D2 ** -0.5
NU1, NU = 16, 24
BLK = 8
WLO = 32

ORDER = list(range(RT, KT)) + list(range(RT))

MISC = (["ln1_0", "v_0", "ln1_1", "v_1"] + [f"cv_{p}" for p in range(8)] + ["wo_0", "ln2_0"]
        + [f"xq_0_{i}" for i in range(HP)] + ["wo_1", "ln2_1"] + [f"xq_1_{i}" for i in range(HP)]
        + [f"xwo_{p}" for p in range(6)] + ["ln3_0", "gate_0"] + [f"xwo_{p}" for p in range(6, 8)]
        + ["wt_0", "ln3_1", "gate_1", "wt_1", "y_0", "y_1"])


def decoder_layer(nc, x, ctxT, attn_w, attn_b, bias_rows, xw_q, xw_k, xw_v, xw_o, gate_w, w_gate, w_up,
                  w_down, consts, rope, selector, out):
    f32, f16, i32 = mybir.dt.float32, mybir.dt.float16, mybir.dt.int32
    ALU, ACT, AX = mybir.AluOpType, mybir.ActivationFunctionType, mybir.AxisListType
    ctx = ExitStack()
    with ctx:
        def sb(name, shape, dt=f32):
            return ctx.enter_context(nc.sbuf_tensor(name, shape, dt))

        def sem(name):
            return ctx.enter_context(nc.semaphore(name))

        x_sb = sb("x_sb", [P, NT, D])
        xb_sb = sb("xb_sb", [P, NT, D])
        x2_sb = sb("x2_sb", [P, NT, D])
        x2b_sb = x_sb
        x3_sb = xb_sb
        xn_sb = sb("xn_sb", [P, TPH, D])
        xnT = sb("xnT", [D, T])
        ctxT_OT = sb("ctxT_OT", [P, T])
        ctxT_sb = ctxT_OT[0:DC, :]
        OT = ctxT_OT
        attn_w_sb = sb("attn_w_sb", [D, 6, D])
        attn_b_sb = sb("attn_b_sb", [D, 5])
        rows_sb = sb("rows_sb", [P, 2, D])
        xwq_sb = sb("xwq_sb", [D, H2 * D2])
        xwk_sb = sb("xwk_sb", [DC, H2 * D2])
        xwv_sb = sb("xwv_sb", [DC, H2 * D2])
        xwo_sb = sb("xwo_sb", [P, HP, D])
        gate_sb = sb("gate_sb", [D, E])
        wg_sb = sb("wg_sb", [D, FT])
        wu_sb = sb("wu_sb", [D, FT])
        wd_sb = sb("wd_sb", [P, KT, D])
        consts_sb = sb("consts_sb", [P, D + HG + 2 + G + E * E])
        ident = consts_sb[:, 0:D]
        mask_h4 = consts_sb[:, D:D + HG]
        mask_h2 = consts_sb[:, D + HG:D + HG + 2]
        mask_g = consts_sb[:, D + HG + 2:D + HG + 2 + G]
        tri = consts_sb[:, D + HG + 2 + G:]
        rope_sb = sb("rope_sb", [D, 2, S])
        sel_sb = sb("sel_sb", [P, RT * P], f16)
        t12 = sb("t12", [D, 2 * HALF])
        t1, t2 = t12[:, 0:HALF], t12[:, HALF:]
        qkr = sb("qkr", [D, 2 * HALF])
        qr, kr = qkr[:, 0:HALF], qkr[:, HALF:]
        qG = sb("qG", [D, G, T])
        kM = sb("kM", [D, B, HG, S])
        VM = sb("VM", [P, 2, NT, G, 2, 32])
        kxM = sb("kxM", [P, HP, B, 2, S])
        Vx = sb("Vx", [P, B, HP, D2])
        qx = sb("qx", [P, HP, HALF])
        mx = sb("mx", [P, 2, BLK])
        NE = 4
        sh = sb("sh", [P, 2, BLK * S])
        ex = sb("ex", [P, NE, BLK * S])
        ls = sb("ls", [P, NE, BLK])
        rs = sb("rs", [P, NE, BLK])
        NPT = 6
        PT = sb("PT", [P, NPT, BLK * S])
        PTx = sb("PTx", [P, 2, BLK, 2, S])
        OTx = t12[:, 0:2 * HP * P].rearrange("p (r k s) -> p r k s", r=2, k=HP)
        st = sb("st", [P, TPH, 6])
        mv = sb("mv", [P, TPH, 2])
        ve = sb("ve", [P, TPH])
        vh = sb("vh", [P, TPH])
        yi = sb("yi", [P, TPH], i32)
        ya = sb("ya", [P, TPH])
        yb = sb("yb", [P, TPH])
        lg = sb("lg", [P, TPH, E])
        lm = sb("lm", [P, TPH])
        gt, eq = (qkr[:, i * TPH * E * E:(i + 1) * TPH * E * E].rearrange("p (n e f) -> p n e f", n=TPH, e=E)
                  for i in range(2))
        rank = sb("rank", [P, TPH, E])
        lsft = sb("lsft", [P, TPH, E])
        lex = sb("lex", [P, TPH, E])
        wk = sb("wk", [P, TPH, E])
        wsum = sb("wsum", [P, TPH])
        wrec = sb("wrec", [P, TPH])
        wte = sb("wte", [P, TPH, E])
        wT = sb("wT", [P, T], f16)
        ffn = qG[:, :, :].rearrange("p g t -> p (g t)").rearrange("p (n t) -> p n t", t=HALF)
        sg, hu, hh = ffn[:, 0:2, :], ffn[:, 2:4, :], ffn[:, 4:7, :]
        yT = qkr[:, HALF:]
        y_sb = x2_sb

        bank = [ctx.enter_context(nc.psum_tensor(f"bank{i}", [P, 512], f32)) for i in range(8)]
        sbank = lambda u: bank[u % 3]
        tbank = lambda u: bank[3 + u % 2]
        pvb = bank[5]
        gbank = lambda u: bank[u % 2]
        ubank = lambda u: bank[2 + u % 2]
        wbank = bank[4]
        rope_bank = [bank[0], bank[1], bank[2], bank[5]]

        ld = {n: sem(f"ld_{n}") for n in ("x", "ctx", "aw", "ab", "rows", "xq", "xk", "xv", "xo", "gw", "wg",
                                          "wu", "wd", "wd2", "cst", "rope", "sel")}
        zeroed = sem("zeroed")
        dve_c = sem("dve_c")
        pool_c = sem("pool_c")
        act_c = sem("act_c")
        misc_full = [sem(f"misc_full{i}") for i in range(2)]
        misc_free = [sem(f"misc_free{i}") for i in range(2)]
        kx_full, kx_free = sem("kx_full"), sem("kx_free")
        rope_full, rope_free = sem("rope_full"), sem("rope_free")
        xn_ready = sem("xn_ready")
        xnT_ready = sem("xnT_ready")
        rot_ready = sem("rot_ready")
        masked = sem("masked")
        vm_ready = sem("vm_ready")
        s_full = sem("s_full")
        s_sub = sem("s_sub")
        e_ready = sem("e_ready")
        r_ready = sem("r_ready")
        p_ready = sem("p_ready")
        t_full = sem("t_full")
        t_copied = sem("t_copied")
        pv_full = sem("pv_full")
        pv_copied = sem("pv_copied")
        cv_ready = sem("cv_ready")
        qx_ready = sem("qx_ready")
        xb_ready = sem("xb_ready")
        lsft_ready, lex_ready = sem("lsft_ready"), sem("lex_ready")
        wte_ready = sem("wte_ready")
        g_full, u_full, w_full = sem("g_full"), sem("u_full"), sem("w_full")
        sg_ready = sem("sg_ready")
        hu_ready = sem("hu_ready")
        h_ready = sem("h_ready")
        down_done = sem("down_done")
        yT_ready = sem("yT_ready")
        y_ready = sem("y_ready")
        stored = sem("stored")

        def misc(name):
            i = MISC.index(name)
            return i % 2, i // 2

        def misc_claim(pe, name):
            b, n = misc(name)
            if n:
                pe.wait_ge(misc_free[b], n)
            return bank[6 + b], misc_full[b]

        def misc_read(eng, name):
            b, n = misc(name)
            eng.wait_ge(misc_full[b], n + 1)
            return bank[6 + b], misc_free[b]

        def rows(k):
            return min(P, FT - k * P)

        block = ctx.enter_context(nc.Block())

        @block.sync
        def _(sp):
            def load(name, dst, src):
                sp.dma_start(dst, src).then_inc(ld[name], 16)

            load("x", x_sb[:], x.rearrange("(n p) d -> p n d", p=P))
            load("cst", consts_sb[:], consts)
            load("ctx", ctxT_sb, ctxT)
            load("xk", xwk_sb[:], xw_k)
            load("aw", attn_w_sb[:], attn_w)
            load("ab", attn_b_sb[:], attn_b)
            load("rope", rope_sb[:], rope)
            load("xv", xwv_sb[:], xw_v)
            load("rows", rows_sb[:], bias_rows.unsqueeze(0).broadcast_to([P, 2, D]))
            load("xq", xwq_sb[:], xw_q)
            load("xo", xwo_sb[:], xw_o)
            load("gw", gate_sb[:], gate_w)
            load("sel", sel_sb[:], selector)
            load("wg", wg_sb[:], w_gate)
            load("wu", wu_sb[:], w_up)
            last = rows(KT - 1)
            load("wd", wd_sb[:, 0:KT - 1, :], w_down[0:(KT - 1) * P].rearrange("(k p) d -> p k d", p=P))
            load("wd2", wd_sb[0:last, KT - 1, :], w_down[(KT - 1) * P:FT])
            for hf in range(2):
                sp.wait_ge(y_ready, hf + 1)
                sp.dma_start(out[hf * HALF:(hf + 1) * HALF].rearrange("(n p) d -> p n d", p=P),
                             y_sb[:, hf * TPH:(hf + 1) * TPH, :]).then_inc(stored, 16)
            sp.wait_ge(stored, 32)

        @block.gpsimd
        def _(pool):
            nc.gpsimd.memset(VM[:], 0.0).then_inc(zeroed, 1)
            nc.gpsimd.memset(PTx[:], 0.0).then_inc(zeroed, 1)
            nc.gpsimd.memset(wT[:], 0.0).then_inc(zeroed, 1)
            pool.wait_ge(ld["x"], 16)
            pool.wait_ge(ld["rows"], 16)
            nc.gpsimd.tensor_tensor(xb_sb[:], x_sb[:], rows_sb[:, 0:1, :].broadcast_to([P, NT, D]),
                                    ALU.add).then_inc(xb_ready, 1)

            def divide(u):
                pool.wait_ge(r_ready, u + 1)
                v = ex[:, u % NE, :].rearrange("p (c t) -> p c t", t=S)
                nc.gpsimd.tensor_tensor(v, v, rs[:, u % NE, :].unsqueeze(2).broadcast_to([P, BLK, S]),
                                        ALU.mult).then_inc(p_ready, 1)

            def x2_bias(hf):
                b, n = misc(f"wo_{hf}")
                pool.wait_ge(misc_free[b], n + 1)
                tl = slice(hf * TPH, (hf + 1) * TPH)
                nc.gpsimd.tensor_tensor(x2b_sb[:, tl, :], x2_sb[:, tl, :],
                                        rows_sb[:, 1:2, :].broadcast_to([P, TPH, D]), ALU.add).then_inc(xb_ready, 1)

            for u in range(NU):
                divide(u)
                if u == 12:
                    x2_bias(0)
                if u == 19:
                    x2_bias(1)

        @block.scalar
        def _(act):
            def copy_kx(i):
                act.wait_ge(kx_full, i + 1)
                if i == 0:
                    act.wait_ge(ld["cst"], 16)
                hp, hf = i // 2, i % 2
                src = bank[3 + i % 2][:, :].rearrange("p (b t) -> p b t", t=S)
                for j in range(2):
                    ins = nc.scalar.activation(kxM[:, hp, hf * BPH:(hf + 1) * BPH, j, :], src, ACT.Copy,
                                               scale=mask_h2[:, j:j + 1])
                ins.then_inc(kx_free, 1)

            def copy_xnT(stage, hf):
                ps, free = misc_read(act, f"ln{stage}_{hf}")
                nc.scalar.copy(xnT[:, hf * HALF:(hf + 1) * HALF], ps[:, :]).then_inc(free, 1)

            def copy_v(hf):
                if hf == 0:
                    act.wait_ge(zeroed, 1)
                ps, free = misc_read(act, f"v_{hf}")
                for b2 in range(2):
                    for h2 in range(2):
                        src = ps[b2 * S:(b2 + 1) * S, :].rearrange("p (n a h d) -> p n a h d", a=2, h=2, d=D1)[:, :, :, h2, :]
                        dst = VM[h2 * S:(h2 + 1) * S, b2, hf * TPH:(hf + 1) * TPH].rearrange(
                            "p n g a c -> p (n g) a c")
                        for a in range(2):
                            col = (2 * a + h2) * D1
                            ins = nc.scalar.copy(dst[:, :, a, col:col + D1], src[:, :, a, :])
                ins.then_inc(free, 1)

            def mask_qk(hf):
                act.wait_ge(rot_ready, hf + 1)
                tok = slice(hf * HALF, (hf + 1) * HALF)
                for g in range(G):
                    nc.scalar.activation(qG[:, g, tok], qr[:, :], ACT.Copy, scale=mask_g[:, g:g + 1])
                for i in range(HG):
                    ins = nc.scalar.activation(kM[:, hf * BPH:(hf + 1) * BPH, i, :],
                                               kr[:, :].rearrange("p (b t) -> p b t", t=S), ACT.Copy,
                                               scale=mask_h4[:, i:i + 1])
                ins.then_inc(masked, 1)

            def exponentials(u):
                act.wait_ge(s_sub, u + 1)
                if u >= NE:
                    act.wait_ge(t_full, u - NE + 1)
                nc.scalar.activation(ex[:, u % NE, :], sh[:, u % 2, :], ACT.Exp,
                                     scale=SCALE1 if u < NU1 else SCALE2).then_inc(e_ready, 1)

            def copy_t(u):
                act.wait_ge(t_full, u + 1)
                if u < NU1:
                    if u >= NPT:
                        act.wait_ge(pv_full, (u - NPT) // 4 + 1)
                    nc.scalar.copy(PT[:, u % NPT, :], tbank(u)[:, :]).then_inc(t_copied, 1)
                else:
                    if u == NU1:
                        act.wait_ge(zeroed, 2)
                    if u >= NU1 + 2:
                        act.wait_ge(pv_full, 4 + u - 2 - NU1 + 1)
                    src = tbank(u)[:, :].rearrange("p (c s) -> p c s", s=S)
                    for j in range(2):
                        r = slice(j * S, (j + 1) * S)
                        ins = nc.scalar.copy(PTx[r, u % 2, :, j, :], src[r])
                    ins.then_inc(t_copied, 1)

            def copy_cv(p):
                ps, free = misc_read(act, f"cv_{p}")
                for b2 in range(2):
                    for h2 in range(2):
                        src = ps[b2 * S:(b2 + 1) * S, :].rearrange("p (n h d) -> p n h d", h=2, d=D2)[:, :, h2, :]
                        ins = nc.scalar.copy(Vx[h2 * S:(h2 + 1) * S, 2 * p + b2, :, :], src)
                ins.then_inc(free, 1)

            def copy_ot(hf):
                act.wait_ge(pv_full, 2 * hf + 2)
                nc.scalar.activation(OT[:, hf * HALF:(hf + 1) * HALF], pvb[:, :], ACT.Identity,
                                     bias=attn_b_sb[:, 4:5]).then_inc(pv_copied, 1)

            def copy_xq(hf):
                if hf:
                    act.wait_ge(s_full, NU1 + TPH)
                for hp in range(HP):
                    ps, free = misc_read(act, f"xq_{hf}_{hp}")
                    nc.scalar.copy(qx[:, hp, :], ps[:, :]).then_inc(free, 1)

            def copy_otx(p):
                act.wait_ge(pv_full, 4 + p + 1)
                if p >= 2:
                    b, n = misc(f"xwo_{p - 2}")
                    act.wait_ge(misc_full[b], n + 1)
                nc.scalar.copy(OTx[:, p % 2, :, :].rearrange("p k s -> p (k s)"), pvb[:, :]).then_inc(pv_copied, 1)

            def router_exp(hf):
                act.wait_ge(lsft_ready, hf + 1)
                if hf:
                    act.wait_ge(wte_ready, hf)
                nc.scalar.activation(lex[:], lsft[:], ACT.Exp).then_inc(lex_ready, 1)

            def silu(u):
                r = rows(ORDER[u % KT])
                act.wait_ge(g_full, u + 1)
                if u >= 2:
                    act.wait_ge(hu_ready, u - 1)
                nc.scalar.activation(sg[0:r, u % 2, :], gbank(u)[0:r, :], ACT.Silu).then_inc(sg_ready, 1)

            def copy_yT(hf):
                act.wait_ge(down_done, KT * (hf + 1))
                if hf:
                    b, n = misc("y_0")
                    act.wait_ge(misc_full[b], n + 1)
                nc.scalar.copy(yT, pvb[:, :]).then_inc(yT_ready, 1)

            for i in range(8):
                copy_kx(i)
            copy_xnT(1, 0)
            act.wait_ge(ld["ab"], 16)
            copy_v(0)
            copy_xnT(1, 1)
            mask_qk(0)
            copy_v(1)
            mask_qk(1)
            for j in range(NU + 4):
                if j < NU:
                    exponentials(j)
                if 2 <= j < NU + 2:
                    copy_t(j - 2)
                if 2 <= j < 10:
                    copy_cv(j - 2)
                if j == 9:
                    copy_ot(0)
                if j == 12:
                    copy_xnT(2, 0)
                    copy_xq(0)
                if j == 17:
                    copy_ot(1)
                if j == 19:
                    copy_xnT(2, 1)
                    copy_xq(1)
                if j - 3 >= NU1 and j - 3 < NU:
                    copy_otx(j - 3 - NU1)
                if j == 24:
                    copy_xnT(3, 0)
                if j == 25:
                    router_exp(0)
            for u in range(2 * KT):
                silu(u)
                if u == 2:
                    copy_xnT(3, 1)
                if u == 5:
                    router_exp(1)
                if u == KT + 1:
                    copy_yT(0)
            copy_yT(1)

        @block.vector
        def _(dve):
            chain = [0]

            def link(ins):
                chain[0] += 1
                ins.then_inc(dve_c, 1)
                dve.wait_ge(dve_c, chain[0])

            def layer_norm(src, hf, k):
                for n in range(TPH):
                    ins = nc.vector.bn_stats(st[:, n, :], src[:, hf * TPH + n, :])
                link(ins)
                for n in range(TPH):
                    ins = nc.vector.bn_aggr(mv[:, n, :], st[:, n, :])
                link(ins)
                link(nc.vector.tensor_scalar(ve[:], mv[:, :, 1], EPS, None, ALU.add))
                link(nc.vector.tensor_scalar(yi[:], ve[:].bitcast(i32), 1, None, ALU.logical_shift_right))
                link(nc.vector.tensor_scalar(ya[:].bitcast(i32), yi[:], -1.0, float(0x5F3759DF), ALU.mult, ALU.add))
                for _ in range(4):
                    link(nc.vector.scalar_tensor_tensor(yb[:], ya[:], -0.5, ya[:], ALU.mult, ALU.mult))
                    link(nc.vector.tensor_tensor(vh[:], yb[:], ve[:], ALU.mult))
                    link(nc.vector.scalar_tensor_tensor(ya[:], vh[:], 1.5, ya[:], ALU.add, ALU.mult))
                if k:
                    b, n = misc(("ln1_0", "ln1_1", "ln2_0", "ln2_1", "ln3_0", "ln3_1")[k - 1])
                    dve.wait_ge(misc_full[b], n + 1)
                for n in range(TPH):
                    ins = nc.vector.tensor_scalar(xn_sb[:, n, :], src[:, hf * TPH + n, :], mv[:, n, 0:1],
                                                  ya[:, n:n + 1], ALU.subtract, ALU.mult)
                ins.then_inc(xn_ready, 1)

            def rotate(hf):
                if hf == 0:
                    dve.wait_ge(ld["rope"], 16)
                    dve.wait_ge(ld["ab"], 16)
                else:
                    dve.wait_ge(masked, hf)
                def table(i):
                    return rope_sb[:, i:i + 1, :].broadcast_to([D, BPH, S])
                for k, dst in ((0, qr), (1, kr)):
                    dve.wait_ge(rope_full, 2 * hf + k + 1)
                    for i, t in ((0, t1), (1, t2)):
                        src = rope_bank[2 * k + i][:, :].rearrange("p (b s) -> p b s", s=S)
                        ins = nc.vector.scalar_tensor_tensor(
                            t[:, :].rearrange("p (b s) -> p b s", s=S), src, attn_b_sb[:, 2 * k + i:2 * k + i + 1],
                            table(i), ALU.add, ALU.mult)
                    ins.then_inc(rope_free, 1)
                    dve.wait_ge(rope_free, 2 * hf + k + 1)
                    ins = nc.vector.tensor_tensor(dst, t1, t2, ALU.add)
                    if k == 0:
                        link(ins)
                    else:
                        ins.then_inc(rot_ready, 1)
                        dve.wait_ge(rot_ready, hf + 1)

            def shift(u):
                dve.wait_ge(s_full, u + 1)
                v = sbank(u)[:, :].rearrange("p (c t) -> p c t", t=S)
                link(nc.vector.reduce_max(mx[:, u % 2, :], v, AX.X))
                if u >= 2:
                    dve.wait_ge(e_ready, u - 1)
                nc.vector.tensor_tensor(sh[:, u % 2, :].rearrange("p (c t) -> p c t", t=S), v,
                                        mx[:, u % 2, :].unsqueeze(2).broadcast_to([P, BLK, S]),
                                        ALU.subtract).then_inc(s_sub, 1)

            def sums(u):
                dve.wait_ge(e_ready, u + 1)
                if u >= NE:
                    dve.wait_ge(p_ready, u - NE + 1)
                link(nc.vector.reduce_sum(ls[:, u % NE, :], ex[:, u % NE, :].rearrange("p (c t) -> p c t", t=S), AX.X))
                nc.vector.reciprocal(rs[:, u % NE, :], ls[:, u % NE, :]).then_inc(r_ready, 1)

            def add_x2(hf):
                dve.wait_ge(xb_ready, 1)
                ps, free = misc_read(dve, f"wo_{hf}")
                tl = slice(hf * TPH, (hf + 1) * TPH)
                nc.vector.tensor_tensor(x2_sb[:, tl, :].rearrange("p n d -> p (n d)"), ps[:, :],
                                        xb_sb[:, tl, :].rearrange("p n d -> p (n d)"), ALU.add).then_inc(free, 1)
                b, n = misc(f"wo_{hf}")
                dve.wait_ge(misc_free[b], n + 1)

            def add_x3(p):
                if p in (0, TPH):
                    dve.wait_ge(xb_ready, 2 + p // TPH)
                ps, free = misc_read(dve, f"xwo_{p}")
                nc.vector.tensor_tensor(x3_sb[:, p, :], ps[:, 0:D], x2b_sb[:, p, :], ALU.add).then_inc(free, 1)
                if p % TPH == TPH - 1:
                    b, n = misc(f"xwo_{p}")
                    dve.wait_ge(misc_free[b], n + 1)
                    b, n = misc(f"xwo_{p - 1}")
                    dve.wait_ge(misc_free[b], n + 1)

            def route(hf):
                ps, free = misc_read(dve, f"gate_{hf}")
                link(nc.vector.tensor_copy(lg[:].rearrange("p n e -> p (n e)"), ps[:, 0:TPH * E]))
                nc.vector.reduce_max(lm[:], ps[:, 0:TPH * E].rearrange("p (n e) -> p n e", e=E), AX.X).then_inc(free, 1)
                b, n = misc(f"gate_{hf}")
                dve.wait_ge(misc_free[b], n + 1)
                if hf:
                    dve.wait_ge(lex_ready, hf)
                nc.vector.tensor_tensor(lsft[:], lg[:], lm[:].unsqueeze(2).broadcast_to([P, TPH, E]),
                                        ALU.subtract).then_inc(lsft_ready, 1)
                other = lg[:].unsqueeze(2).broadcast_to([P, TPH, E, E])
                own = lg[:].unsqueeze(3).broadcast_to([P, TPH, E, E])
                nc.vector.tensor_tensor(gt, other, own, ALU.is_gt)
                link(nc.vector.tensor_tensor(eq, other, own, ALU.is_equal))
                eqf = eq.rearrange("p n e f -> p n (e f)")
                link(nc.vector.tensor_tensor(eqf, eqf, tri.unsqueeze(1).broadcast_to([P, TPH, E * E]), ALU.mult))
                link(nc.vector.tensor_tensor(gt, gt, eq, ALU.add))
                link(nc.vector.reduce_sum(rank[:], gt, AX.X))
                dve.wait_ge(lex_ready, hf + 1)
                link(nc.vector.scalar_tensor_tensor(wk[:], rank[:], 1.5, lex[:], ALU.is_lt, ALU.mult))
                link(nc.vector.reduce_sum(wsum[:], wk[:], AX.X))
                link(nc.vector.reciprocal(wrec[:], wsum[:]))
                if hf:
                    b, n = misc("wt_0")
                    dve.wait_ge(misc_full[b], n + 1)
                nc.vector.tensor_tensor(wte[:], wk[:], wrec[:].unsqueeze(2).broadcast_to([P, TPH, E]),
                                        ALU.mult).then_inc(wte_ready, 1)
                dve.wait_ge(wte_ready, hf + 1)

            def split_wT(hf):
                if hf == 0:
                    dve.wait_ge(zeroed, 3)
                ps, free = misc_read(dve, f"wt_{hf}")
                tok = slice(hf * HALF, (hf + 1) * HALF)
                link(nc.vector.tensor_copy(wT[0:E, tok], ps[0:E, :]))
                nc.vector.tensor_tensor(wT[WLO:WLO + E, tok], ps[0:E, :], wT[0:E, tok], ALU.subtract).then_inc(free, 1)
                b, n = misc(f"wt_{hf}")
                dve.wait_ge(misc_free[b], n + 1)

            def hidden(u):
                k = ORDER[u % KT]
                r = rows(k)
                dve.wait_ge(sg_ready, u + 1)
                dve.wait_ge(u_full, u + 1)
                if u >= 3:
                    dve.wait_ge(down_done, u - 2)
                routed = k < RT
                dst = hu[0:r, u % 2, :] if routed else hh[0:r, u % 3, :]
                nc.vector.tensor_tensor(dst, ubank(u)[0:r, :], sg[0:r, u % 2, :], ALU.mult).then_inc(hu_ready, 1)
                dve.wait_ge(hu_ready, u + 1)
                if routed:
                    dve.wait_ge(w_full, (u // KT) * RT + u % KT - (KT - RT) + 1)
                    nc.vector.tensor_tensor(hh[:, u % 3, :], wbank[:, :], hu[:, u % 2, :], ALU.mult).then_inc(h_ready, 1)
                else:
                    dve.sem_inc(h_ready, 1)

            def add_y(hf):
                ps, free = misc_read(dve, f"y_{hf}")
                tl = slice(hf * TPH, (hf + 1) * TPH)
                nc.vector.tensor_tensor(y_sb[:, tl, :].rearrange("p n d -> p (n d)"), ps[:, :],
                                        x3_sb[:, tl, :].rearrange("p n d -> p (n d)"), ALU.add).then_inc(y_ready, 1)

            dve.wait_ge(ld["x"], 16)
            layer_norm(x_sb, 0, 0)
            layer_norm(x_sb, 1, 1)
            rotate(0)
            rotate(1)
            for j in range(NU + 4):
                if j < NU:
                    shift(j)
                if 1 <= j < NU + 1:
                    sums(j - 1)
                if j in (11, 18):
                    hf = j // 18
                    add_x2(hf)
                    layer_norm(x2_sb, hf, 2 + hf)
                if 0 <= j - 4 - NU1 < NT:
                    add_x3(j - 4 - NU1)
                    if j - 4 - NU1 == TPH - 1:
                        layer_norm(x3_sb, 0, 4)
                if j == 25:
                    route(0)
            for u in range(2 * KT):
                hidden(u)
                if u == 1:
                    layer_norm(x3_sb, 1, 5)
                    split_wT(0)
                if u == 4:
                    route(1)
                if u == 9:
                    split_wT(1)
                if u == KT + 2:
                    add_y(0)
            add_y(1)

        @block.tensor
        def _(pe):
            mm = nc.tensor.matmul

            def context_keys(i):
                hp, hf = i // 2, i % 2
                if i == 0:
                    pe.wait_ge(ld["ctx"], 16)
                    pe.wait_ge(ld["xk"], 16)
                if i >= 2:
                    pe.wait_ge(kx_free, i - 1)
                mm(bank[3 + i % 2][:, :], xwk_sb[:, hp * P:(hp + 1) * P], ctxT_sb[:, hf * HALF:(hf + 1) * HALF],
                   start=True, stop=True).then_inc(kx_full, 1)

            def transpose_xn(stage, hf):
                ps, full = misc_claim(pe, f"ln{stage}_{hf}")
                if stage == 1 and hf == 0:
                    pe.wait_ge(ld["cst"], 16)
                pe.wait_ge(xn_ready, 2 * (stage - 1) + hf + 1)
                for n in range(TPH):
                    ins = nc.tensor.transpose(ps[:, n * P:(n + 1) * P], xn_sb[:, n, :], ident)
                ins.then_inc(full, 1)

            def xnT_wait(stage, hf):
                b, n = misc(f"ln{stage}_{hf}")
                pe.wait_ge(misc_free[b], n + 1)

            def queries_keys(hf):
                if hf == 0:
                    pe.wait_ge(ld["aw"], 16)
                xnT_wait(1, hf)
                tok = slice(hf * HALF, (hf + 1) * HALF)
                for k in range(2):
                    if hf:
                        pe.wait_ge(rope_free, k + 1)
                    for i in range(2):
                        ins = mm(rope_bank[2 * k + i][:, :], attn_w_sb[:, 2 * k + i, :], xnT[:, tok],
                                 start=True, stop=True)
                    ins.then_inc(rope_full, 1)

            def values(hf):
                ps, full = misc_claim(pe, f"v_{hf}")
                for n in range(TPH):
                    ins = mm(ps[:, n * P:(n + 1) * P], xnT[:, (hf * TPH + n) * P:(hf * TPH + n + 1) * P],
                             attn_w_sb[:, 4, :], start=True, stop=True)
                ins.then_inc(full, 1)

            def context_values(p):
                ps, full = misc_claim(pe, f"cv_{p}")
                if p == 0:
                    pe.wait_ge(ld["xv"], 16)
                mm(ps[:, :], ctxT_sb[:, p * P:(p + 1) * P], xwv_sb[:, :], start=True, stop=True).then_inc(full, 1)

            def scores(u):
                if u < 3:
                    pe.wait_ge(rope_free, 4)
                else:
                    pe.wait_ge(s_sub, u - 2)
                if u < NU1:
                    quad, g = u // 4, u % 4
                    if g == 0:
                        pe.wait_ge(masked, quad // 2 + 1)
                    for pp in range(2):
                        for b2 in range(2):
                            b = 4 * quad + 2 * pp + b2
                            ins = mm(sbank(u)[b2 * S:(b2 + 1) * S, pp * HG * S:(pp + 1) * HG * S],
                                     qG[:, g, b * S:(b + 1) * S], kM[:, b].rearrange("p i t -> p (i t)"),
                                     start=True, stop=True)
                else:
                    p = u - NU1
                    if p % TPH == 0:
                        for hp in range(HP - 2, HP):
                            b, n = misc(f"xq_{p // TPH}_{hp}")
                            pe.wait_ge(misc_free[b], n + 1)
                    if p == 0:
                        pe.wait_ge(kx_free, 8)
                    for hp in range(HP):
                        for b2 in range(2):
                            b = 2 * p + b2
                            ins = mm(sbank(u)[b2 * S:(b2 + 1) * S, hp * P:(hp + 1) * P],
                                     qx[:, hp, (b % BPH) * S:(b % BPH + 1) * S], kxM[:, hp, b].rearrange("p j t -> p (j t)"),
                                     start=True, stop=True)
                ins.then_inc(s_full, 1)

            def transpose_p(u):
                pe.wait_ge(p_ready, u + 1)
                if u == 0:
                    pe.wait_ge(kx_free, 7)
                elif u == 1:
                    pe.wait_ge(kx_free, 8)
                else:
                    pe.wait_ge(t_copied, u - 1)
                for c in range(4):
                    ins = nc.tensor.transpose(tbank(u)[:, c * P:(c + 1) * P], ex[:, u % NE, c * P:(c + 1) * P], ident)
                ins.then_inc(t_full, 1)

            def attend(quad):
                pe.wait_ge(t_copied, 4 * quad + 4)
                if quad % 2 == 0:
                    b, n = misc(f"v_{quad // 2}" if quad else "v_1")
                    pe.wait_ge(misc_free[b], n + 1)
                    b, n = misc("v_0")
                    pe.wait_ge(misc_free[b], n + 1)
                if quad == 2:
                    pe.wait_ge(pv_copied, 1)
                for pp in range(2):
                    for b2 in range(2):
                        tile = 2 * quad + pp
                        col = (quad % 2) * 4 * S + (2 * pp + b2) * S
                        for a in range(2):
                            for g in range(G):
                                ptg = PT[:, (4 * quad + g) % NPT, :].rearrange("p (c s) -> p c s", s=S)
                                ins = mm(pvb[32 * g:32 * (g + 1), col:col + S], VM[:, b2, tile, g, a, :],
                                         ptg[:, (2 * pp + a) * 2 + b2, :], start=(a == 0), stop=(a == 1),
                                         skip_group_check=True)
                ins.then_inc(pv_full, 1)

            def project_o(hf):
                ps, full = misc_claim(pe, f"wo_{hf}")
                pe.wait_ge(pv_copied, hf + 1)
                for n in range(TPH):
                    t = (hf * TPH + n) * P
                    ins = mm(ps[:, n * P:(n + 1) * P], OT[:, t:t + P], attn_w_sb[:, 5, :], start=True, stop=True)
                ins.then_inc(full, 1)

            def cross_queries(hf):
                if hf == 0:
                    pe.wait_ge(ld["xq"], 16)
                xnT_wait(2, hf)
                for hp in range(HP):
                    ps, full = misc_claim(pe, f"xq_{hf}_{hp}")
                    mm(ps[:, :], xwq_sb[:, hp * P:(hp + 1) * P], xnT[:, hf * HALF:(hf + 1) * HALF],
                       start=True, stop=True).then_inc(full, 1)

            def cross_attend(p):
                u = NU1 + p
                pe.wait_ge(t_copied, u + 1)
                pe.wait_ge(pv_copied, 2 + p)
                if p == 0:
                    for q in (6, 7):
                        b, n = misc(f"cv_{q}")
                        pe.wait_ge(misc_free[b], n + 1)
                o = pvb[:, :].rearrange("p (j h b s) -> p j h b s", j=2, h=2, b=2)
                for j in range(2):
                    for b2 in range(2):
                        for c in range(2):
                            hp = 2 * j + c
                            ins = mm(o[c * S:(c + 1) * S, j, :, b2, :], Vx[:, 2 * p + b2, hp, :],
                                     PTx[:, u % 2, 2 * hp + b2, :, :], start=True, stop=True)
                ins.then_inc(pv_full, 1)

            def cross_project(p):
                if p == 0:
                    pe.wait_ge(ld["xo"], 16)
                ps, full = misc_claim(pe, f"xwo_{p}")
                pe.wait_ge(pv_copied, 2 + p + 1)
                for k in range(HP):
                    ins = mm(ps[:, 0:D], OTx[:, p % 2, k, :], xwo_sb[:, k, :], start=(k == 0), stop=(k == HP - 1))
                ins.then_inc(full, 1)

            def gate(hf):
                ps, full = misc_claim(pe, f"gate_{hf}")
                if hf == 0:
                    pe.wait_ge(ld["gw"], 16)
                xnT_wait(3, hf)
                for n in range(TPH):
                    t = (hf * TPH + n) * P
                    ins = mm(ps[:, n * E:(n + 1) * E], xnT[:, t:t + P], gate_sb[:, :], start=True, stop=True)
                ins.then_inc(full, 1)

            def transpose_w(hf):
                ps, full = misc_claim(pe, f"wt_{hf}")
                pe.wait_ge(wte_ready, hf + 1)
                for n in range(TPH):
                    ins = nc.tensor.transpose(ps[0:E, n * P:(n + 1) * P], wte[:, n, :], ident)
                ins.then_inc(full, 1)

            def expert_up(u):
                hf, k = u // KT, ORDER[u % KT]
                r = rows(k)
                tok = slice(hf * HALF, (hf + 1) * HALF)
                if u == 0:
                    pe.wait_ge(ld["wg"], 16)
                    pe.wait_ge(ld["wu"], 16)
                    pe.wait_ge(s_sub, NU)
                    pe.wait_ge(t_copied, NU)
                if u >= 2:
                    pe.wait_ge(sg_ready, u - 1)
                mm(gbank(u)[0:r, :], wg_sb[:, k * P:k * P + r], xnT[:, tok], start=True, stop=True).then_inc(g_full, 1)
                if u >= 2:
                    pe.wait_ge(hu_ready, u - 1)
                mm(ubank(u)[0:r, :], wu_sb[:, k * P:k * P + r], xnT[:, tok], start=True, stop=True).then_inc(u_full, 1)

            def spread_w(u):
                hf, k = u // KT, ORDER[u % KT]
                if k >= RT:
                    return
                if u % KT == KT - RT:
                    b, n = misc(f"wt_{hf}")
                    pe.wait_ge(misc_free[b], n + 1)
                    if hf == 0:
                        pe.wait_ge(ld["sel"], 16)
                pe.wait_ge(h_ready, u)
                mm(wbank[:, :], sel_sb[:, k * P:(k + 1) * P], wT[:, hf * HALF:(hf + 1) * HALF],
                   start=True, stop=True).then_inc(w_full, 1)

            def expert_down(u):
                hf, k = u // KT, ORDER[u % KT]
                r = rows(k)
                if u == 0:
                    pe.wait_ge(ld["wd"], 16)
                    pe.wait_ge(ld["wd2"], 16)
                    pe.wait_ge(pv_copied, 2 + NT)
                if u == KT:
                    pe.wait_ge(yT_ready, 1)
                pe.wait_ge(h_ready, u + 1)
                mm(pvb[:, :], wd_sb[0:r, k, :], hh[0:r, u % 3, :], start=(u % KT == 0),
                   stop=(u % KT == KT - 1)).then_inc(down_done, 1)

            def transpose_y(hf):
                ps, full = misc_claim(pe, f"y_{hf}")
                pe.wait_ge(yT_ready, hf + 1)
                for n in range(TPH):
                    ins = nc.tensor.transpose(ps[:, n * P:(n + 1) * P], yT[:, n * P:(n + 1) * P], ident)
                ins.then_inc(full, 1)

            for i in range(8):
                context_keys(i)
            transpose_xn(1, 0)
            queries_keys(0)
            values(0)
            transpose_xn(1, 1)
            queries_keys(1)
            values(1)
            for u in range(3):
                scores(u)
            for i in range(NU):
                transpose_p(i)
                if i < 8:
                    context_values(i)
                if i == 17:
                    transpose_xn(2, 1)
                    cross_queries(1)
                if i + 3 < NU:
                    scores(i + 3)
                if i in (3, 7, 11, 15):
                    attend(i // 4)
                if i == 9:
                    project_o(0)
                if i == 10:
                    transpose_xn(2, 0)
                    cross_queries(0)
                if i == 16:
                    project_o(1)
                if i - 1 >= NU1:
                    cross_attend(i - 1 - NU1)
                if i - 2 >= NU1:
                    cross_project(i - 2 - NU1)
            transpose_xn(3, 0)
            gate(0)
            cross_attend(NT - 1)
            cross_project(NT - 2)
            cross_project(NT - 1)
            for u in range(2 * KT):
                if u == 3:
                    transpose_w(0)
                    transpose_xn(3, 1)
                    gate(1)
                if u == 10:
                    transpose_w(1)
                expert_up(u)
                spread_w(u)
                if u:
                    expert_down(u - 1)
                if u == KT + 2:
                    transpose_y(0)
            expert_down(2 * KT - 1)
            transpose_y(1)


def _tables():
    f = np.float32
    row = np.arange(P)
    ident = np.eye(P, dtype=f)
    mask_h4 = (row[:, None] // D1 % HG == np.arange(HG)).astype(f)
    mask_h2 = (row[:, None] // S == np.arange(2)).astype(f)
    mask_g = (row[:, None] // (HG * D1) == np.arange(G)).astype(f)
    tri = np.broadcast_to((np.arange(E)[None, :] < np.arange(E)[:, None]).astype(f).reshape(1, E * E), (P, E * E))
    consts = np.concatenate([ident, mask_h4, mask_h2, mask_g, tri], axis=1)
    inv_freq = (f(1.0) / f(10000.0) ** (np.arange(0, D1, 2, dtype=f) / f(D1))).astype(f)
    freqs = (np.arange(S, dtype=f)[None, :] * inv_freq[row % D1 % 4][:, None]).astype(f)
    sign = np.where(row % D1 < D1 // 2, -1.0, 1.0).astype(f)[:, None]
    rope = np.stack([np.cos(freqs), sign * np.sin(freqs)], axis=1).astype(f)
    selector = np.zeros((P, RT * P), np.float16)
    feature = np.arange(RT * P)
    selector[feature // F, feature] = 1
    selector[WLO + feature // F, feature] = 1
    return consts, rope, selector


def kernel(**inputs):
    import concourse.bacc as _bacc
    from concourse.bass_utils import run_bass_kernel_spmd as _run

    a = {k: np.asarray(v) for k, v in inputs.items()}
    heads = np.arange(D).reshape(H1, D1)
    straight = heads[:, [0, 2, 4, 6, 1, 3, 5, 7]].reshape(-1)
    swapped = heads[:, [1, 3, 5, 7, 0, 2, 4, 6]].reshape(-1)
    wq, wk, wv, wo = (a[f"L0_attn_W{n}"] for n in "qkvo")
    bq, bk, bv, bo = (a[f"L0_attn_b{n}"] for n in "qkvo")
    consts, rope, selector = _tables()
    arrays = {
        "x": a["x"].reshape(T, D),
        "ctxT": a["ctx_768"].reshape(T, DC).T,
        "attn_w": np.stack([wq[straight].T, wq[swapped].T, wk[straight].T, wk[swapped].T, wv.T, wo.T], axis=1),
        "attn_b": np.stack([bq[straight], bq[swapped], bk[straight], bk[swapped], bv], axis=1),
        "bias_rows": np.stack([bo, a["L0_xattn_bo"]]),
        "xw_q": a["L0_xattn_Wq"], "xw_k": a["L0_xattn_Wk"], "xw_v": a["L0_xattn_Wv"],
        "xw_o": a["L0_xattn_Wo"].reshape(2, 2, 2, D2, D).transpose(1, 3, 0, 2, 4).reshape(P, HP, D),
        "gate_w": a["L0_ffn_gate_w"],
        "w_gate": np.concatenate([a["L0_ffn_exp_gate"], a["L0_ffn_sh_gate"]]).transpose(1, 0, 2).reshape(D, FT),
        "w_up": np.concatenate([a["L0_ffn_exp_up"], a["L0_ffn_sh_up"]]).transpose(1, 0, 2).reshape(D, FT),
        "w_down": np.concatenate([a["L0_ffn_exp_down"], a["L0_ffn_sh_down"]]).reshape(FT, D),
        "consts": consts, "rope": rope, "selector": selector,
    }
    arrays = {f"{k}_dram": np.ascontiguousarray(v) for k, v in arrays.items()}
    nc = _bacc.Bacc("TRN2", target_bir_lowering=False, num_devices=1)
    args = [nc.dram_tensor(k, v.shape, mybir.dt.from_np(v.dtype), kind="ExternalInput").ap()
            for k, v in arrays.items()]
    out = nc.dram_tensor("out_dram", (T, D), mybir.dt.float32, kind="ExternalOutput").ap()
    decoder_layer(nc, *args, out)
    r = _run(nc, [arrays], core_ids=[0])
    return r.results[0]["out_dram"].reshape(B, S, D)
```

```python
from contextlib import ExitStack

import numpy as np
import concourse.bass as bass
from concourse import mybir

P = 128
B, S, D = 16, 64, 128
T = B * S
NT = T // P
HALF = T // 2
TPH = NT // 2
BPH = B // 2
H1, D1 = 16, 8
G, HG = 4, 4
H2, D2 = 8, 64
HP = H2 // 2
DC = 96
E, F, NSH = 8, 176, 2
FT = (E + NSH) * F
KT = -(-FT // P)
RT = E * F // P
assert RT * P == E * F
EPS = 1e-5
SCALE1, SCALE2 = D1 ** -0.5, D2 ** -0.5
NU1, NU = 16, 24
BLK = 8
WLO = 32

ORDER = list(range(RT, KT)) + list(range(RT)) + list(range(RT)) + list(range(RT, KT))

MISC = (["ln1_0", "q_0", "k_0", "ln1_1", "q_1", "k_1", "v_0", "cv_0", "cv_1", "q_2", "k_2", "v_1",
         "q_3", "k_3", "cv_2", "cv_3", "wo_0", "ln2_0", "kx_4"]
        + [f"xq_0_{i}" for i in range(HP)] + ["kx_5", "wo_1", "kx_6", "kx_7", "ln2_1", "cv_4"]
        + [f"xq_1_{i}" for i in range(HP)] + ["xwo_0", "cv_5", "xwo_1", "cv_6", "xwo_2", "cv_7"]
        + [f"xwo_{p}" for p in range(3, 6)] + ["ln3_0", "xwo_6", "gate_0", "xwo_7"]
        + ["wt_0", "ln3_1", "gate_1", "wt_1", "y_0", "y_1"])
LN = ["ln1_0", "ln1_1", "ln2_0", "ln2_1", "ln3_0", "ln3_1"]


def decoder_layer(nc, x, ctxT, attn_w, attn_b, bias_rows, xw_q, xw_k, xw_v, xw_o, gate_w, w_gate, w_up,
                  w_down, consts, rope, selector, out):
    f32, f16, i32 = mybir.dt.float32, mybir.dt.float16, mybir.dt.int32
    ALU, ACT, AX = mybir.AluOpType, mybir.ActivationFunctionType, mybir.AxisListType
    ctx = ExitStack()
    with ctx:
        def sb(name, shape, dt=f32):
            return ctx.enter_context(nc.sbuf_tensor(name, shape, dt))

        def sem(name):
            return ctx.enter_context(nc.semaphore(name))

        x_sb = sb("x_sb", [P, NT, D])
        xb_sb = sb("xb_sb", [P, NT, D])
        x2_sb = sb("x2_sb", [P, NT, D])
        x2b_sb = x_sb
        x3_sb = xb_sb
        xn_sb = sb("xn_sb", [P, 2, TPH, D])
        xnT = sb("xnT", [D, 2, T], f16)
        ctxT_sb = sb("ctxT_sb", [P, T])
        attn_w_sb = sb("attn_w_sb", [D, 2, 5, D], f16)
        wo_sb = sb("wo_sb", [D, D])
        attn_b_sb = sb("attn_b_sb", [D, 5])
        rows_sb = sb("rows_sb", [P, 2, D])
        xwq_sb = sb("xwq_sb", [D, 2, H2 * D2], f16)
        CH = H2 * D2
        xwk_sb = sb("xwk_sb", [P, CH])
        xwv_sb = sb("xwv_sb", [P, CH])
        stage = [sb(f"stage{i}", [P, CH]) for i in range(2)]
        xwo_sb = sb("xwo_sb", [P, HP, D])
        gate_raw = sb("gate_raw", [D, E])
        gate_sb = sb("gate_sb", [D, 2, E], f16)
        wg_sb = sb("wg_sb", [D, 2, FT], f16)
        wu_sb = sb("wu_sb", [D, 2, FT], f16)
        wd_sb = sb("wd_sb", [P, 2, KT * D], f16)
        consts_sb = sb("consts_sb", [P, D + HG + 2 + G + E * E + 2 * 32])
        ident = consts_sb[:, 0:D]
        mask_h4 = consts_sb[:, D:D + HG]
        mask_h2 = consts_sb[:, D + HG:D + HG + 2]
        mask_g = consts_sb[:, D + HG + 2:D + HG + 2 + G]
        tri = consts_sb[:, D + HG + 2 + G:D + HG + 2 + G + E * E]
        ones_h = consts_sb[:, D + HG + 2 + G + E * E:].rearrange("p (a c) -> p a c", a=2)
        rope_sb = sb("rope_sb", [D, 2, S])
        sel_sb = sb("sel_sb", [P, RT * P], f16)
        QT = 4 * S
        t12 = sb("t12", [D, 2 * HALF])
        OT = t12
        qkr = sb("qkr", [D, 2 * HALF])
        qr, kr = (qkr[:, :].rearrange("p (r k t) -> p r k t", r=2, k=2)[:, :, i, :] for i in range(2))
        qG = sb("qG", [D, G, T])
        kM = sb("kM", [D, B, HG, S])
        VM = sb("VM", [P, 2, NT, G, 2, 32])
        kxM = sb("kxM", [P, HP, B, 2, S])
        Vx = sb("Vx", [P, B, HP, D2])
        qx = qG
        mx = sb("mx", [P, 2, BLK])
        NE = 4
        sh = sb("sh", [P, 2, BLK * S])
        ex = sb("ex", [P, NE, BLK * S])
        ls = sb("ls", [P, NE, BLK])
        rs = sb("rs", [P, NE, BLK])
        rsum = sb("rsum", [P, QT])
        NPT = 6
        PT = sb("PT", [P, NPT, BLK * S])
        PTx = sb("PTx", [P, 2, BLK, 2, S])
        OTx = t12[:, 0:2 * HP * P].rearrange("p (r k s) -> p r k s", r=2, k=HP)
        st = sb("st", [P, TPH, 6])
        mv = sb("mv", [P, 2, TPH, 2])
        ve = sb("ve", [P, 2, TPH])
        rstd = sb("rstd", [P, 2, TPH])
        minus_half = sb("minus_half", [P, TPH])
        lg = sb("lg", [P, TPH, E])
        lm = sb("lm", [P, TPH])
        gt, eq = (qkr[:, i * TPH * E * E:(i + 1) * TPH * E * E].rearrange("p (n e f) -> p n e f", n=TPH, e=E)
                  for i in range(2))
        rank = sb("rank", [P, TPH, E])
        lsft = sb("lsft", [P, TPH, E])
        lex = sb("lex", [P, TPH, E])
        wk = sb("wk", [P, TPH, E])
        wsum = sb("wsum", [P, TPH])
        wrec = sb("wrec", [P, TPH])
        wte = sb("wte", [P, TPH, E])
        wT = sb("wT", [P, T], f16)
        ffn = qG[:, :, :].rearrange("p g t -> p (g t)").rearrange("p (n t) -> p n t", t=HALF)
        sg, hu, hh = ffn[:, 0:2, :], ffn[:, 2:4, :], ffn[:, 4:6, :]
        hs = ffn[:, 6:8, :].bitcast(f16).rearrange("p r (i t) -> p r i t", i=2)
        raw = qG[:, :, :].rearrange("p g t -> p (g t)")
        attn_raw, xwq_raw = raw[:, 0:5 * D], raw[:, 5 * D:5 * D + CH]
        yT = qkr[:, HALF:]
        y_sb = x2_sb

        bank = [ctx.enter_context(nc.psum_tensor(f"bank{i}", [P, 512], f32)) for i in range(8)]
        sbank = lambda u: bank[u % 3]
        tbank = lambda u: bank[3 + u % 2]
        kxbank = lambda i: bank[min(3 + i, 5)]
        pvb = bank[5]
        gbank = lambda u: bank[u % 2]
        ubank = lambda u: bank[2 + u % 2]
        wbank = bank[4]

        ld = {n: sem(f"ld_{n}") for n in ("x0", "x1", "ctx", "aw", "wo", "ab", "rows", "xq", "xk", "xv", "xo", "gw",
                                          "cst", "rope", "sel")}
        chunk_in = [sem(f"chunk_in{i}") for i in range(2)]
        chunk_hi = sem("chunk_hi")
        chunk_lo = sem("chunk_lo")
        aw_hi, aw_lo = sem("aw_hi"), sem("aw_lo")
        padded = sem("padded")
        zeroed = sem("zeroed")
        dve_c = sem("dve_c")
        pool_c = sem("pool_c")
        act_c = sem("act_c")
        misc_full = [sem(f"misc_full{i}") for i in range(2)]
        misc_free = [sem(f"misc_free{i}") for i in range(2)]
        gw_split = sem("gw_split")
        kx_full, kx_free = sem("kx_full"), sem("kx_free")
        xn_ready = sem("xn_ready")
        var_ready = sem("var_ready")
        rstd_ready = sem("rstd_ready")
        xnT_hi = sem("xnT_hi")
        rot_ready = sem("rot_ready")
        q_masked = sem("q_masked")
        k_masked = sem("k_masked")
        vm_ready = sem("vm_ready")
        s_full = sem("s_full")
        s_sub = sem("s_sub")
        e_ready = sem("e_ready")
        r_ready = sem("r_ready")
        p_ready = sem("p_ready")
        t_full = sem("t_full")
        t_copied = sem("t_copied")
        pv_full = sem("pv_full")
        pv_copied = sem("pv_copied")
        ot_ready = sem("ot_ready")
        cv_ready = sem("cv_ready")
        qx_ready = sem("qx_ready")
        xb_ready = sem("xb_ready")
        lsft_ready, lex_ready = sem("lsft_ready"), sem("lex_ready")
        wte_ready = sem("wte_ready")
        g_full, u_full, w_full = sem("g_full"), sem("u_full"), sem("w_full")
        sg_ready = sem("sg_ready")
        hu_ready = sem("hu_ready")
        h_ready = sem("h_ready")
        h_hi = sem("h_hi")
        h_lo = sem("h_lo")
        down_done = sem("down_done")
        yT_ready = sem("yT_ready")
        y_ready = sem("y_ready")
        stored = sem("stored")

        def misc(name):
            i = MISC.index(name)
            return i % 2, i // 2

        def misc_claim(pe, name):
            b, n = misc(name)
            if n:
                pe.wait_ge(misc_free[b], n)
            return bank[6 + b], misc_full[b]

        def misc_read(eng, name):
            b, n = misc(name)
            eng.wait_ge(misc_full[b], n + 1)
            return bank[6 + b], misc_free[b]

        def routed_before(u):
            return sum(k < RT for k in ORDER[:u])

        def rows(k):
            return min(P, FT - k * P)

        CHUNKS = []
        for src, dst in ((w_gate, wg_sb), (w_up, wu_sb)):
            CHUNKS += [(src[:, c:min(c + CH, FT)], dst, D, slice(c, min(c + CH, FT))) for c in range(0, FT, CH)]
        for k in range(0, KT - 1, CH // D):
            n = min(CH // D, KT - 1 - k)
            CHUNKS.append((w_down[k * P:(k + n) * P].rearrange("(k p) d -> p k d", p=P), wd_sb, P,
                           slice(k * D, (k + n) * D)))
        CHUNK_AT = [3, 4, 5, 6, 10, 11, 12, 13, 14, 20, 21, 22, 23]
        assert len(CHUNK_AT) == len(CHUNKS) + 1
        last = FT - (KT - 1) * P
        CHUNKS.append((w_down[(KT - 1) * P:FT], wd_sb, last, slice((KT - 1) * D, KT * D)))

        def landed(eng, c):
            eng.wait_ge(chunk_in[c % 2], 16 * (c // 2 + 1))

        block = ctx.enter_context(nc.Block())

        @block.sync
        def _(sp):
            def load(name, dst, src):
                sp.dma_start(dst, src).then_inc(ld[name], 16)

            def load_x(hf):
                sp.dma_start(x_sb[:, hf * TPH:(hf + 1) * TPH, :],
                             x[hf * HALF:(hf + 1) * HALF].rearrange("(n p) d -> p n d", p=P)).then_inc(ld[f"x{hf}"], 16)

            load_x(0)
            load("xk", xwk_sb[0:DC, :], xw_k)
            load("aw", attn_raw, attn_w.rearrange("p k d -> p (k d)")[:, 0:5 * D])
            load_x(1)
            load("rope", rope_sb[:], rope)
            load("xv", xwv_sb[0:DC, :], xw_v)
            load("xq", xwq_raw, xw_q)
            load("rows", rows_sb[:], bias_rows.unsqueeze(0).broadcast_to([P, 2, D]))
            load("wo", wo_sb[:], attn_w[:, 5, :])
            load("xo", xwo_sb[:], xw_o)
            load("gw", gate_raw[:], gate_w)
            load("sel", sel_sb[:], selector)
            for c, (src, _, r, cols) in enumerate(CHUNKS):
                if c >= 2:
                    sp.wait_ge(chunk_lo, c - 1)
                dst = stage[c % 2][0:r, 0:cols.stop - cols.start]
                if len(src.shape) == 3:
                    dst = dst.rearrange("p (k d) -> p k d", d=D)
                sp.dma_start(dst, src).then_inc(chunk_in[c % 2], 16)
            for hf in range(2):
                sp.wait_ge(y_ready, hf + 1)
                sp.dma_start(out[hf * HALF:(hf + 1) * HALF].rearrange("(n p) d -> p n d", p=P),
                             y_sb[:, hf * TPH:(hf + 1) * TPH, :]).then_inc(stored, 16)
            sp.wait_ge(stored, 32)

        @block.gpsimd
        def _(pool):
            def rest(dst, src, k):
                pool.wait_ge(aw_hi, k)
                nc.gpsimd.tensor_tensor(dst[1], src, dst[0], ALU.subtract).then_inc(aw_lo, 1)

            def inverse_std(k):
                pool.wait_ge(var_ready, k + 1)
                if k >= 2:
                    pool.wait_ge(xn_ready, k - 1)
                nc.gpsimd.tensor_scalar(ve[:, k % 2, :], mv[:, k % 2, :, 1], EPS, None, ALU.add).then_inc(pool_c, 1)
                pool.wait_ge(pool_c, k + 2)
                nc.gpsimd.tensor_tensor(rstd[:, k % 2, :], ve[:, k % 2, :], minus_half[:],
                                        ALU.pow).then_inc(rstd_ready, 1)

            def rotated(quad):
                for name in "qk":
                    b, n = misc(f"{name}_{quad}")
                    pool.wait_ge(misc_free[b], n + 1)
                pool.wait_ge(q_masked, G * (quad - 1))
                t = t12[:, :].rearrange("p (k i t) -> p k i t", k=2, i=2)
                nc.gpsimd.tensor_tensor(qkr[:, quad % 2 * HALF:(quad % 2 + 1) * HALF].rearrange(
                    "p (k t) -> p k t", k=2), t[:, :, 0, :], t[:, :, 1, :], ALU.add).then_inc(rot_ready, 1)

            def mask_k(quad):
                pool.wait_ge(rot_ready, quad + 1)
                nc.gpsimd.tensor_tensor(
                    kM[:, 4 * quad:4 * quad + 4],
                    kr[:, quad % 2, :].rearrange("p (b t) -> p b t", t=S).unsqueeze(2).broadcast_to([D, 4, HG, S]),
                    mask_h4.unsqueeze(1).unsqueeze(3).broadcast_to([D, 4, HG, S]), ALU.mult).then_inc(k_masked, 1)

            def split_chunk(c):
                _, dst, r, cols = CHUNKS[c]
                pool.wait_ge(chunk_hi, c + 1)
                nc.gpsimd.tensor_tensor(dst[0:r, 1, cols], stage[c % 2][0:r, 0:cols.stop - cols.start],
                                        dst[0:r, 0, cols], ALU.subtract).then_inc(chunk_lo, 1)

            def split_h(u):
                r = rows(ORDER[u])
                pool.wait_ge(h_hi, u + 1)
                nc.gpsimd.tensor_tensor(hs[0:r, u % 2, 1, :], hh[0:r, u % 2, :], hs[0:r, u % 2, 0, :],
                                        ALU.subtract).then_inc(h_lo, 1)

            def divide(u):
                pool.wait_ge(r_ready, u - NU1 + 1)
                v = ex[:, u % NE, :].rearrange("p (c t) -> p c t", t=S)
                nc.gpsimd.tensor_tensor(v, v, rs[:, u % NE, :].unsqueeze(2).broadcast_to([P, BLK, S]),
                                        ALU.mult).then_inc(p_ready, 1)

            def x2_bias(hf):
                b, n = misc(f"wo_{hf}")
                pool.wait_ge(misc_free[b], n + 1)
                tl = slice(hf * TPH, (hf + 1) * TPH)
                nc.gpsimd.tensor_tensor(x2b_sb[:, tl, :], x2_sb[:, tl, :],
                                        rows_sb[:, 1:2, :].broadcast_to([P, TPH, D]), ALU.add).then_inc(xb_ready, 1)

            nc.gpsimd.memset(minus_half[:], -0.5).then_inc(pool_c, 1)
            pool.wait_ge(pool_c, 1)
            inverse_std(0)
            rest([attn_w_sb[:, i].rearrange("p k d -> p (k d)") for i in range(2)], attn_raw, 1)
            inverse_std(1)
            rest([xwq_sb[:, i] for i in range(2)], xwq_raw, 2)
            nc.gpsimd.memset(VM[:], 0.0).then_inc(zeroed, 1)
            nc.gpsimd.memset(wT[:], 0.0).then_inc(zeroed, 1)
            pool.wait_ge(ld["rows"], 16)
            pool.wait_ge(xn_ready, 2)
            nc.gpsimd.tensor_tensor(xb_sb[:], x_sb[:], rows_sb[:, 0:1, :].broadcast_to([P, NT, D]),
                                    ALU.add).then_inc(xb_ready, 1)
            nc.gpsimd.memset(PTx[:], 0.0).then_inc(zeroed, 1)
            rotated(2)
            mask_k(2)
            for c in range(3):
                split_chunk(c)
            rotated(3)
            mask_k(3)
            for c in range(3, 8):
                split_chunk(c)
            inverse_std(2)
            split_chunk(8)
            x2_bias(0)
            for u in range(NU1, NU):
                divide(u)
                if u == 16:
                    inverse_std(3)
                if u == 19:
                    x2_bias(1)
                if u == 23:
                    inverse_std(4)
                if 20 <= u <= 23:
                    split_chunk(u - 11)
            inverse_std(5)
            for u in range(2 * KT - 2):
                split_h(u)

        @block.scalar
        def _(act):
            def copy_kx(i):
                hp, hf = i % HP, i // HP
                if hf == 0:
                    act.wait_ge(kx_full, i + 1)
                    ps, free = kxbank(i), kx_free
                else:
                    ps, free = misc_read(act, f"kx_{i}")
                if i == 0:
                    act.wait_ge(ld["cst"], 16)
                src = ps[:, :].rearrange("p (b t) -> p b t", t=S)
                for j in range(2):
                    ins = nc.scalar.activation(kxM[:, hp, hf * BPH:(hf + 1) * BPH, j, :], src, ACT.Copy,
                                               scale=mask_h2[:, j:j + 1])
                ins.then_inc(free, 1)

            def split_weights(dst, src, name):
                act.wait_ge(ld[name], 16)
                nc.scalar.copy(dst, src).then_inc(aw_hi, 1)

            def chunk_float16(c):
                _, dst, r, cols = CHUNKS[c]
                landed(act, c)
                nc.scalar.copy(dst[0:r, 0, cols], stage[c % 2][0:r, 0:cols.stop - cols.start]).then_inc(chunk_hi, 1)

            def copy_xnT(stage, hf):
                ps, _ = misc_read(act, f"ln{stage}_{hf}")
                nc.scalar.copy(xnT[:, 0, hf * HALF:(hf + 1) * HALF], ps[:, :]).then_inc(xnT_hi, 1)

            def copy_v(hf):
                if hf == 0:
                    act.wait_ge(zeroed, 1)
                ps, free = misc_read(act, f"v_{hf}")
                for b2 in range(2):
                    for h2 in range(2):
                        src = ps[b2 * S:(b2 + 1) * S, :].rearrange("p (n a h d) -> p n a h d", a=2, h=2, d=D1)[:, :, :, h2, :]
                        dst = VM[h2 * S:(h2 + 1) * S, b2, hf * TPH:(hf + 1) * TPH].rearrange(
                            "p n g a c -> p (n g) a c")
                        for a in range(2):
                            col = (2 * a + h2) * D1
                            ins = nc.scalar.copy(dst[:, :, a, col:col + D1], src[:, :, a, :])
                ins.then_inc(free, 1)

            def mask_q(quad):
                act.wait_ge(rot_ready, quad + 1)
                if quad == 0:
                    act.wait_ge(aw_lo, 2)
                for g in range(G):
                    nc.scalar.activation(qG[:, g, quad * QT:(quad + 1) * QT], qr[:, quad % 2, :], ACT.Copy,
                                         scale=mask_g[:, g:g + 1]).then_inc(q_masked, 1)
            def exponentials(u):
                act.wait_ge(s_sub, u + 1)
                if u >= NE:
                    act.wait_ge(t_full, u - NE + 1)
                nc.scalar.activation(ex[:, u % NE, :], sh[:, u % 2, :], ACT.Exp,
                                     scale=SCALE1 if u < NU1 else SCALE2).then_inc(e_ready, 1)

            def copy_t(u):
                act.wait_ge(t_full, u + 1)
                if u < NU1:
                    if u >= NPT:
                        act.wait_ge(pv_full, (u - NPT) // 4 + 1)
                    nc.scalar.copy(PT[:, u % NPT, :], tbank(u)[:, :]).then_inc(t_copied, 1)
                else:
                    if u == NU1:
                        act.wait_ge(zeroed, 3)
                    if u >= NU1 + 2:
                        act.wait_ge(pv_full, 4 + u - 2 - NU1 + 1)
                    src = tbank(u)[:, :].rearrange("p (c s) -> p c s", s=S)
                    for j in range(2):
                        r = slice(j * S, (j + 1) * S)
                        ins = nc.scalar.copy(PTx[r, u % 2, :, j, :], src[r])
                    ins.then_inc(t_copied, 1)

            def copy_cv(p):
                ps, free = misc_read(act, f"cv_{p}")
                for b2 in range(2):
                    for h2 in range(2):
                        src = ps[b2 * S:(b2 + 1) * S, :].rearrange("p (n h d) -> p n h d", h=2, d=D2)[:, :, h2, :]
                        ins = nc.scalar.copy(Vx[h2 * S:(h2 + 1) * S, 2 * p + b2, :, :], src)
                ins.then_inc(free, 1)

            def bias_ot(quad):
                act.wait_ge(pv_copied, quad + 1)
                o = OT[:, quad * QT:(quad + 1) * QT]
                nc.scalar.activation(o, o, ACT.Identity, bias=attn_b_sb[:, 4:5]).then_inc(ot_ready, 1)

            def copy_xq(hf):
                act.wait_ge(s_full, NU1 if hf else NU1 // 2)
                for hp in range(HP):
                    ps, free = misc_read(act, f"xq_{hf}_{hp}")
                    nc.scalar.copy(qx[:, hp, hf * HALF:(hf + 1) * HALF], ps[:, :]).then_inc(free, 1)

            def copy_otx(p):
                act.wait_ge(pv_full, 4 + p + 1)
                if p >= 2:
                    b, n = misc(f"xwo_{p - 2}")
                    act.wait_ge(misc_full[b], n + 1)
                nc.scalar.copy(OTx[:, p % 2, :, :].rearrange("p k s -> p (k s)"), pvb[:, :]).then_inc(pv_copied, 1)

            def router_exp(hf):
                act.wait_ge(lsft_ready, hf + 1)
                if hf:
                    act.wait_ge(wte_ready, hf)
                nc.scalar.activation(lex[:], lsft[:], ACT.Exp).then_inc(lex_ready, 1)

            def silu(u):
                r = rows(ORDER[u])
                act.wait_ge(g_full, u + 1)
                if u >= 2:
                    act.wait_ge(hu_ready, u - 1)
                nc.scalar.activation(sg[0:r, u % 2, :], gbank(u)[0:r, :], ACT.Silu).then_inc(sg_ready, 1)

            def h_float16(u):
                r = rows(ORDER[u])
                act.wait_ge(h_ready, u + 1)
                if u >= 2:
                    act.wait_ge(down_done, u - 1)
                nc.scalar.copy(hs[0:r, u % 2, 0, :], hh[0:r, u % 2, :]).then_inc(h_hi, 1)

            def copy_yT(hf):
                act.wait_ge(down_done, KT * (hf + 1))
                if hf:
                    b, n = misc("y_0")
                    act.wait_ge(misc_full[b], n + 1)
                nc.scalar.copy(yT, pvb[:, :]).then_inc(yT_ready, 1)

            act.dma_start(ctxT_sb[0:DC, :], ctxT).then_inc(ld["ctx"], 16)
            act.dma_start(consts_sb[:], consts).then_inc(ld["cst"], 16)
            act.dma_start(attn_b_sb[:], attn_b).then_inc(ld["ab"], 16)
            split_weights(attn_w_sb[:, 0].rearrange("p k d -> p (k d)"), attn_raw, "aw")
            copy_xnT(1, 0)
            split_weights(xwq_sb[:, 0], xwq_raw, "xq")
            copy_kx(0)
            copy_kx(1)
            copy_xnT(1, 1)
            mask_q(0)
            copy_kx(2)
            for j in range(NU + 4):
                if j == 16:
                    copy_t(14)
                    copy_t(15)
                if j == 17:
                    bias_ot(3)
                if j < NU:
                    exponentials(j)
                if j == 0:
                    copy_v(0)
                    mask_q(1)
                if j in (1, 2):
                    copy_cv(j - 1)
                if j in (9, 12, 15):
                    bias_ot(j // 3 - 3)
                if 2 <= j < NU + 2 and not 16 <= j <= 19:
                    copy_t(j - 2)
                if j == 4:
                    mask_q(2)
                if j == 3:
                    copy_kx(3)
                if j == 5:
                    copy_v(1)
                if j in (8, 11):
                    copy_cv((j - 2) // 3)
                if j == 9:
                    mask_q(3)
                if j == 14:
                    copy_xnT(2, 0)
                if j == 15:
                    copy_kx(4)
                    copy_xq(0)
                if j == 16:
                    copy_kx(5)
                if j == 18:
                    copy_kx(6)
                    copy_t(16)
                    copy_kx(7)
                if j == 19:
                    copy_xnT(2, 1)
                    copy_t(17)
                if j == 25:
                    copy_xnT(3, 0)
                if j - 3 >= NU1 and j - 3 < NU:
                    copy_otx(j - 3 - NU1)
                if j == 19:
                    copy_cv(4)
                    copy_xq(1)
                if 21 <= j <= 23:
                    copy_cv(j - 16)
                if j == 27:
                    router_exp(0)
                if j in CHUNK_AT:
                    chunk_float16(CHUNK_AT.index(j))
            for u in range(2 * KT + 1):
                if u < 2 * KT:
                    silu(u)
                if u:
                    h_float16(u - 1)
                if u == 3:
                    copy_xnT(3, 1)
                if u == 6:
                    router_exp(1)
                if u == KT + 1:
                    copy_yT(0)
            copy_yT(1)

        @block.vector
        def _(dve):
            chain = [0]

            def link(ins):
                chain[0] += 1
                ins.then_inc(dve_c, 1)
                dve.wait_ge(dve_c, chain[0])

            def statistics(k, src):
                hf = k % 2
                for n in range(TPH):
                    ins = nc.vector.bn_stats(st[:, n, :], src[:, hf * TPH + n, :])
                link(ins)
                for n in range(TPH):
                    ins = nc.vector.bn_aggr(mv[:, hf, n, :], st[:, n, :])
                ins.then_inc(var_ready, 1)
                dve.wait_ge(var_ready, k + 1)

            def normalise(k, src):
                hf = k % 2
                dve.wait_ge(rstd_ready, k + 1)
                if k >= 2:
                    b, n = misc(LN[k - 2])
                    dve.wait_ge(misc_full[b], n + 1)
                for n in range(TPH):
                    ins = nc.vector.tensor_scalar(xn_sb[:, hf, n, :], src[:, hf * TPH + n, :], mv[:, hf, n, 0:1],
                                                  rstd[:, hf, n:n + 1], ALU.subtract, ALU.mult)
                ins.then_inc(xn_ready, 1)

            def rest_xnT(k):
                tok = slice(k % 2 * HALF, (k % 2 + 1) * HALF)
                ps, free = misc_read(dve, LN[k])
                dve.wait_ge(xnT_hi, k + 1)
                nc.vector.tensor_tensor(xnT[:, 1, tok], ps[:, :], xnT[:, 0, tok], ALU.subtract).then_inc(free, 1)

            def rotate(quad, names="qk"):
                if quad == 0:
                    dve.wait_ge(ld["rope"], 16)
                    dve.wait_ge(ld["ab"], 16)
                if quad >= 1:
                    dve.wait_ge(rot_ready, quad)
                for k, name in ((0, "q"), (1, "k")):
                    if name not in names:
                        continue
                    ps, free = misc_read(dve, f"{name}_{quad}")
                    for i in range(2):
                        ins = nc.vector.scalar_tensor_tensor(
                            t12[:, (2 * k + i) * QT:(2 * k + i + 1) * QT].rearrange("p (b s) -> p b s", s=S),
                            ps[:, i * QT:(i + 1) * QT].rearrange("p (b s) -> p b s", s=S),
                            attn_b_sb[:, 2 * k + i:2 * k + i + 1],
                            rope_sb[:, i:i + 1, :].broadcast_to([D, 4, S]), ALU.add, ALU.mult)
                    ins.then_inc(free, 1)
                if quad >= 2:
                    return
                for name in "qk":
                    b, n = misc(f"{name}_{quad}")
                    dve.wait_ge(misc_free[b], n + 1)
                t = t12[:, :].rearrange("p (k i t) -> p k i t", k=2, i=2)
                nc.vector.tensor_tensor(qkr[:, quad % 2 * HALF:(quad % 2 + 1) * HALF].rearrange(
                    "p (k t) -> p k t", k=2), t[:, :, 0, :], t[:, :, 1, :], ALU.add).then_inc(rot_ready, 1)
                dve.wait_ge(rot_ready, quad + 1)

            def mask_k(quad):
                if quad == 0:
                    dve.wait_ge(ld["cst"], 16)
                for i in range(HG):
                    ins = nc.vector.tensor_scalar(kM[:, 4 * quad:4 * quad + 4, i, :],
                                                  kr[:, quad % 2, :].rearrange("p (b t) -> p b t", t=S),
                                                  mask_h4[:, i:i + 1], None, ALU.mult)
                ins.then_inc(k_masked, 1)
                dve.wait_ge(k_masked, quad + 1)

            def shift(u):
                dve.wait_ge(s_full, u + 1)
                v = sbank(u)[:, :].rearrange("p (c t) -> p c t", t=S)
                link(nc.vector.reduce_max(mx[:, u % 2, :], v, AX.X))
                if u >= 2:
                    dve.wait_ge(e_ready, u - 1)
                nc.vector.tensor_tensor(sh[:, u % 2, :].rearrange("p (c t) -> p c t", t=S), v,
                                        mx[:, u % 2, :].unsqueeze(2).broadcast_to([P, BLK, S]),
                                        ALU.subtract).then_inc(s_sub, 1)

            def sums(u):
                dve.wait_ge(e_ready, u + 1)
                if u >= NU1 + NE:
                    dve.wait_ge(p_ready, u - NU1 - NE + 1)
                link(nc.vector.reduce_sum(ls[:, u % NE, :], ex[:, u % NE, :].rearrange("p (c t) -> p c t", t=S), AX.X))
                nc.vector.reciprocal(rs[:, u % NE, :], ls[:, u % NE, :]).then_inc(r_ready, 1)

            def divide_ot(quad):
                dve.wait_ge(pv_full, quad + 1)
                link(nc.vector.reciprocal(rsum[:], pvb[:, QT:2 * QT]))
                if quad == 0:
                    dve.wait_ge(rot_ready, 4)
                nc.vector.tensor_tensor(OT[:, quad * QT:(quad + 1) * QT], pvb[:, 0:QT], rsum[:],
                                        ALU.mult).then_inc(pv_copied, 1)
                dve.wait_ge(pv_copied, quad + 1)

            def add_x2(hf):
                dve.wait_ge(xb_ready, 1)
                ps, free = misc_read(dve, f"wo_{hf}")
                tl = slice(hf * TPH, (hf + 1) * TPH)
                nc.vector.tensor_tensor(x2_sb[:, tl, :].rearrange("p n d -> p (n d)"), ps[:, :],
                                        xb_sb[:, tl, :].rearrange("p n d -> p (n d)"), ALU.add).then_inc(free, 1)
                b, n = misc(f"wo_{hf}")
                dve.wait_ge(misc_free[b], n + 1)

            def add_x3(p):
                if p in (0, TPH):
                    dve.wait_ge(xb_ready, 2 + p // TPH)
                ps, free = misc_read(dve, f"xwo_{p}")
                nc.vector.tensor_tensor(x3_sb[:, p, :], ps[:, 0:D], x2b_sb[:, p, :], ALU.add).then_inc(free, 1)
                if p % TPH == TPH - 1:
                    b, n = misc(f"xwo_{p}")
                    dve.wait_ge(misc_free[b], n + 1)
                    b, n = misc(f"xwo_{p - 1}")
                    dve.wait_ge(misc_free[b], n + 1)

            def route_shift(hf):
                ps, free = misc_read(dve, f"gate_{hf}")
                link(nc.vector.tensor_copy(lg[:].rearrange("p n e -> p (n e)"), ps[:, 0:TPH * E]))
                nc.vector.reduce_max(lm[:], ps[:, 0:TPH * E].rearrange("p (n e) -> p n e", e=E), AX.X).then_inc(free, 1)
                b, n = misc(f"gate_{hf}")
                dve.wait_ge(misc_free[b], n + 1)
                if hf:
                    dve.wait_ge(lex_ready, hf)
                nc.vector.tensor_tensor(lsft[:], lg[:], lm[:].unsqueeze(2).broadcast_to([P, TPH, E]),
                                        ALU.subtract).then_inc(lsft_ready, 1)

            def route_compare():
                other = lg[:].unsqueeze(2).broadcast_to([P, TPH, E, E])
                own = lg[:].unsqueeze(3).broadcast_to([P, TPH, E, E])
                nc.vector.tensor_tensor(gt, other, own, ALU.is_gt)
                link(nc.vector.tensor_tensor(eq, other, own, ALU.is_equal))

            def route_rank():
                eqf = eq.rearrange("p n e f -> p n (e f)")
                link(nc.vector.tensor_tensor(eqf, eqf, tri.unsqueeze(1).broadcast_to([P, TPH, E * E]), ALU.mult))
                link(nc.vector.tensor_tensor(gt, gt, eq, ALU.add))
                link(nc.vector.reduce_sum(rank[:], gt, AX.X))

            def route_weights(hf):
                dve.wait_ge(lex_ready, hf + 1)
                link(nc.vector.scalar_tensor_tensor(wk[:], rank[:], 1.5, lex[:], ALU.is_lt, ALU.mult))
                link(nc.vector.reduce_sum(wsum[:], wk[:], AX.X))
                link(nc.vector.reciprocal(wrec[:], wsum[:]))
                if hf:
                    b, n = misc("wt_0")
                    dve.wait_ge(misc_full[b], n + 1)
                nc.vector.tensor_tensor(wte[:], wk[:], wrec[:].unsqueeze(2).broadcast_to([P, TPH, E]),
                                        ALU.mult).then_inc(wte_ready, 1)
                dve.wait_ge(wte_ready, hf + 1)

            def split_wT(hf):
                if hf == 0:
                    dve.wait_ge(zeroed, 2)
                ps, free = misc_read(dve, f"wt_{hf}")
                tok = slice(hf * HALF, (hf + 1) * HALF)
                link(nc.vector.tensor_copy(wT[0:E, tok], ps[0:E, :]))
                nc.vector.tensor_tensor(wT[WLO:WLO + E, tok], ps[0:E, :], wT[0:E, tok], ALU.subtract).then_inc(free, 1)
                b, n = misc(f"wt_{hf}")
                dve.wait_ge(misc_free[b], n + 1)

            def hidden(u):
                k = ORDER[u]
                r = rows(k)
                dve.wait_ge(sg_ready, u + 1)
                dve.wait_ge(u_full, u + 1)
                if u >= 2:
                    dve.wait_ge(h_lo, u - 1)
                routed = k < RT
                dst = hu[0:r, u % 2, :] if routed else hh[0:r, u % 2, :]
                nc.vector.tensor_tensor(dst, ubank(u)[0:r, :], sg[0:r, u % 2, :], ALU.mult).then_inc(hu_ready, 1)
                dve.wait_ge(hu_ready, u + 1)
                if routed:
                    dve.wait_ge(w_full, routed_before(u) + 1)
                    nc.vector.tensor_tensor(hh[:, u % 2, :], wbank[:, :], hu[:, u % 2, :], ALU.mult).then_inc(h_ready, 1)
                else:
                    dve.sem_inc(h_ready, 1)

            def rest_h(u):
                r = rows(ORDER[u])
                dve.wait_ge(h_hi, u + 1)
                dve.wait_ge(h_lo, u)
                nc.vector.tensor_tensor(hs[0:r, u % 2, 1, :], hh[0:r, u % 2, :], hs[0:r, u % 2, 0, :],
                                        ALU.subtract).then_inc(h_lo, 1)

            def add_y(hf):
                ps, free = misc_read(dve, f"y_{hf}")
                tl = slice(hf * TPH, (hf + 1) * TPH)
                nc.vector.tensor_tensor(y_sb[:, tl, :].rearrange("p n d -> p (n d)"), ps[:, :],
                                        x3_sb[:, tl, :].rearrange("p n d -> p (n d)"), ALU.add).then_inc(y_ready, 1)

            for t in (ctxT_sb, xwk_sb, xwv_sb):
                nc.vector.memset(t[DC:P, :], 0.0).then_inc(padded, 1)
            dve.wait_ge(ld["x0"], 16)
            statistics(0, x_sb)
            normalise(0, x_sb)
            dve.wait_ge(ld["x1"], 16)
            statistics(1, x_sb)
            rest_xnT(0)
            normalise(1, x_sb)
            rotate(0)
            mask_k(0)
            rest_xnT(1)
            for j in range(NU + 4):
                if j < NU:
                    shift(j)
                if NU1 < j < NU and j != 20:
                    sums(j - 1)
                if j == NU - 1:
                    sums(j)
                if j == 17:
                    add_x2(1)
                    statistics(3, x2_sb)
                if j == 1:
                    rotate(1)
                    mask_k(1)
                if j == 2:
                    rotate(2, "q")
                if j == 3:
                    rotate(2, "k")
                if j == 8:
                    rotate(3, "q")
                    rotate(3, "k")
                if j == 10:
                    dve.wait_ge(ld["gw"], 16)
                    nc.vector.tensor_copy(gate_sb[:, 0, :], gate_raw[:]).then_inc(gw_split, 1)
                    dve.wait_ge(gw_split, 1)
                    nc.vector.tensor_tensor(gate_sb[:, 1, :], gate_raw[:], gate_sb[:, 0, :],
                                            ALU.subtract).then_inc(gw_split, 1)
                if j == 9:
                    divide_ot(0)
                if j == 12:
                    divide_ot(1)
                if j == 14:
                    add_x2(0)
                    statistics(2, x2_sb)
                if j == 15:
                    normalise(2, x2_sb)
                    divide_ot(2)
                    rest_xnT(2)
                if j == 16:
                    divide_ot(3)
                if j == 18:
                    normalise(3, x2_sb)
                if j == 19:
                    sums(19)
                    rest_xnT(3)
                if 0 <= j - 4 - NU1 < NT:
                    add_x3(j - 4 - NU1)
                if j == 23:
                    statistics(4, x3_sb)
                if j == 24:
                    normalise(4, x3_sb)
                if j == 25:
                    rest_xnT(4)
                if j == 26:
                    route_shift(0)
                    route_compare()
                    route_rank()
                    route_weights(0)
            statistics(5, x3_sb)
            for u in range(2 * KT):
                hidden(u)
                if u == 0:
                    normalise(5, x3_sb)
                if u == 1:
                    split_wT(0)
                if u == 3:
                    rest_xnT(5)
                if u == 5:
                    route_shift(1)
                if u == 6:
                    route_compare()
                if u == 7:
                    route_rank()
                if u == 8:
                    route_weights(1)
                if u == 11:
                    split_wT(1)
                if u == KT + 3:
                    add_y(0)
                if u == 2 * KT - 1:
                    rest_h(u - 1)
            rest_h(2 * KT - 1)
            add_y(1)

        @block.tensor
        def _(pe):
            mm = nc.tensor.matmul
            claimed = [0]

            def claim(name):
                assert MISC[claimed[0]] == name, (MISC[claimed[0]], name)
                claimed[0] += 1
                return misc_claim(pe, name)

            def mm3(ps, w, x, start=True, stop=True):
                mm(ps, w[0], x[0], start=start, stop=False)
                mm(ps, w[0], x[1], start=False, stop=False)
                return mm(ps, w[1], x[0], start=False, stop=stop)

            def tokens(a, b):
                return xnT[:, 0, a:b], xnT[:, 1, a:b]

            def context_keys(i):
                hp, hf = i % HP, i // HP
                if i == 0:
                    pe.wait_ge(ld["ctx"], 16)
                    pe.wait_ge(ld["xk"], 16)
                    pe.wait_ge(padded, 3)
                if hf == 0:
                    if i == 3:
                        pe.wait_ge(kx_free, 3)
                    ps, full = kxbank(i), kx_full
                else:
                    ps, full = claim(f"kx_{i}")
                mm(ps[:, :], xwk_sb[:, hp * P:(hp + 1) * P], ctxT_sb[:, hf * HALF:(hf + 1) * HALF],
                   start=True, stop=True).then_inc(full, 1)

            def transpose_xn(stage, hf):
                ps, full = claim(f"ln{stage}_{hf}")
                if stage == 1 and hf == 0:
                    pe.wait_ge(ld["cst"], 16)
                pe.wait_ge(xn_ready, 2 * (stage - 1) + hf + 1)
                for n in range(TPH):
                    ins = nc.tensor.transpose(ps[:, n * P:(n + 1) * P], xn_sb[:, hf, n, :], ident)
                ins.then_inc(full, 1)

            def xnT_wait(stage, hf):
                b, n = misc(f"ln{stage}_{hf}")
                pe.wait_ge(misc_free[b], n + 1)

            def queries_keys(quad):
                if quad == 0:
                    pe.wait_ge(aw_lo, 1)
                xnT_wait(1, quad // 2)
                for k, name in enumerate("qk"):
                    ps, full = claim(f"{name}_{quad}")
                    for i in range(2):
                        ins = mm3(ps[:, i * QT:(i + 1) * QT], [attn_w_sb[:, s, 2 * k + i, :] for s in range(2)],
                                  tokens(quad * QT, (quad + 1) * QT))
                    ins.then_inc(full, 1)

            def values(hf):
                xnT_wait(1, hf)
                ps, full = claim(f"v_{hf}")
                for n in range(TPH):
                    t = (hf * TPH + n) * P
                    ins = mm3(ps[:, n * P:(n + 1) * P], tokens(t, t + P), [attn_w_sb[:, s, 4, :] for s in range(2)])
                ins.then_inc(full, 1)

            def context_values(p):
                ps, full = claim(f"cv_{p}")
                if p == 0:
                    pe.wait_ge(ld["xv"], 16)
                mm(ps[:, :], ctxT_sb[:, p * P:(p + 1) * P], xwv_sb[:, :], start=True, stop=True).then_inc(full, 1)

            def scores(u):
                if u >= 3:
                    pe.wait_ge(s_sub, u - 2)
                if u < NU1:
                    quad, g = u // 4, u % 4
                    pe.wait_ge(q_masked, u + 1)
                    if g == 0:
                        pe.wait_ge(k_masked, quad + 1)
                    for pp in range(2):
                        for b2 in range(2):
                            b = 4 * quad + 2 * pp + b2
                            ins = mm(sbank(u)[b2 * S:(b2 + 1) * S, pp * HG * S:(pp + 1) * HG * S],
                                     qG[:, g, b * S:(b + 1) * S], kM[:, b].rearrange("p i t -> p (i t)"),
                                     start=True, stop=True)
                else:
                    p = u - NU1
                    if p % TPH == 0:
                        for hp in range(HP - 2, HP):
                            b, n = misc(f"xq_{p // TPH}_{hp}")
                            pe.wait_ge(misc_free[b], n + 1)
                    if p == TPH:
                        for i in (2 * HP - 2, 2 * HP - 1):
                            b, n = misc(f"kx_{i}")
                            pe.wait_ge(misc_free[b], n + 1)
                    for hp in range(HP):
                        for b2 in range(2):
                            b = 2 * p + b2
                            ins = mm(sbank(u)[b2 * S:(b2 + 1) * S, hp * P:(hp + 1) * P],
                                     qx[:, hp, b * S:(b + 1) * S], kxM[:, hp, b].rearrange("p j t -> p (j t)"),
                                     start=True, stop=True)
                ins.then_inc(s_full, 1)

            def transpose_p(u):
                if u < NU1:
                    pe.wait_ge(e_ready, u + 1)
                else:
                    pe.wait_ge(p_ready, u - NU1 + 1)
                if u < 2:
                    pe.wait_ge(kx_free, u + 1)
                if u >= 2:
                    pe.wait_ge(t_copied, u - 1)
                for c in range(4):
                    ins = nc.tensor.transpose(tbank(u)[:, c * P:(c + 1) * P], ex[:, u % NE, c * P:(c + 1) * P], ident)
                ins.then_inc(t_full, 1)

            def attend(quad):
                pe.wait_ge(t_copied, 4 * quad + 4)
                if quad % 2 == 0:
                    b, n = misc(f"v_{quad // 2}")
                    pe.wait_ge(misc_free[b], n + 1)
                if quad == 0:
                    pe.wait_ge(kx_free, HP)
                else:
                    pe.wait_ge(pv_copied, quad)
                for pp in range(2):
                    for b2 in range(2):
                        tile = 2 * quad + pp
                        col = (2 * pp + b2) * S
                        for what in range(2):
                            for a in range(2):
                                for g in range(G):
                                    ptg = PT[:, (4 * quad + g) % NPT, :].rearrange("p (c s) -> p c s", s=S)
                                    ins = mm(pvb[32 * g:32 * (g + 1), what * QT + col:what * QT + col + S],
                                             ones_h[:, a, :] if what else VM[:, b2, tile, g, a, :],
                                             ptg[:, (2 * pp + a) * 2 + b2, :], start=(a == 0), stop=(a == 1),
                                             skip_group_check=True)
                ins.then_inc(pv_full, 1)

            def project_o(hf):
                ps, full = claim(f"wo_{hf}")
                pe.wait_ge(ot_ready, 2 * hf + 2)
                if hf == 0:
                    pe.wait_ge(ld["wo"], 16)
                for n in range(TPH):
                    t = (hf * TPH + n) * P
                    ins = mm(ps[:, n * P:(n + 1) * P], OT[:, t:t + P], wo_sb[:, :], start=True, stop=True)
                ins.then_inc(full, 1)

            def cross_queries(hf):
                if hf == 0:
                    pe.wait_ge(aw_lo, 2)
                xnT_wait(2, hf)
                for hp in range(HP):
                    ps, full = claim(f"xq_{hf}_{hp}")
                    mm3(ps[:, :], [xwq_sb[:, s, hp * P:(hp + 1) * P] for s in range(2)],
                        tokens(hf * HALF, (hf + 1) * HALF)).then_inc(full, 1)

            def cross_attend(p):
                u = NU1 + p
                pe.wait_ge(t_copied, u + 1)
                pe.wait_ge(pv_copied, 4 + p)
                b, n = misc(f"cv_{p}")
                pe.wait_ge(misc_free[b], n + 1)
                o = pvb[:, :].rearrange("p (j h b s) -> p j h b s", j=2, h=2, b=2)
                for j in range(2):
                    for b2 in range(2):
                        for c in range(2):
                            hp = 2 * j + c
                            ins = mm(o[c * S:(c + 1) * S, j, :, b2, :], Vx[:, 2 * p + b2, hp, :],
                                     PTx[:, u % 2, 2 * hp + b2, :, :], start=True, stop=True)
                ins.then_inc(pv_full, 1)

            def cross_project(p):
                if p == 0:
                    pe.wait_ge(ld["xo"], 16)
                ps, full = claim(f"xwo_{p}")
                pe.wait_ge(pv_copied, 4 + p + 1)
                for k in range(HP):
                    ins = mm(ps[:, 0:D], OTx[:, p % 2, k, :], xwo_sb[:, k, :], start=(k == 0), stop=(k == HP - 1))
                ins.then_inc(full, 1)

            def gate(hf):
                ps, full = claim(f"gate_{hf}")
                if hf == 0:
                    pe.wait_ge(gw_split, 2)
                xnT_wait(3, hf)
                for n in range(TPH):
                    t = (hf * TPH + n) * P
                    ins = mm3(ps[:, n * E:(n + 1) * E], tokens(t, t + P), [gate_sb[:, s, :] for s in range(2)])
                ins.then_inc(full, 1)

            def transpose_w(hf):
                ps, full = claim(f"wt_{hf}")
                pe.wait_ge(wte_ready, hf + 1)
                for n in range(TPH):
                    ins = nc.tensor.transpose(ps[0:E, n * P:(n + 1) * P], wte[:, n, :], ident)
                ins.then_inc(full, 1)

            def expert_up(u):
                hf, k = u // KT, ORDER[u]
                r = rows(k)
                x = tokens(hf * HALF, (hf + 1) * HALF)
                if u == 0:
                    pe.wait_ge(chunk_lo, len(CHUNKS))
                    pe.wait_ge(s_sub, NU)
                    pe.wait_ge(t_copied, NU)
                if u == KT:
                    xnT_wait(3, 1)
                if u >= 2:
                    pe.wait_ge(sg_ready, u - 1)
                mm3(gbank(u)[0:r, :], [wg_sb[:, s, k * P:k * P + r] for s in range(2)], x).then_inc(g_full, 1)
                if u >= 2:
                    pe.wait_ge(hu_ready, u - 1)
                mm3(ubank(u)[0:r, :], [wu_sb[:, s, k * P:k * P + r] for s in range(2)], x).then_inc(u_full, 1)

            def spread_w(u):
                hf, k = u // KT, ORDER[u]
                if k >= RT:
                    return
                if routed_before(u) == hf * RT:
                    b, n = misc(f"wt_{hf}")
                    pe.wait_ge(misc_free[b], n + 1)
                    if hf == 0:
                        pe.wait_ge(ld["sel"], 16)
                pe.wait_ge(h_ready, u)
                mm(wbank[:, :], sel_sb[:, k * P:(k + 1) * P], wT[:, hf * HALF:(hf + 1) * HALF],
                   start=True, stop=True).then_inc(w_full, 1)

            def expert_down(u):
                hf, k = u // KT, ORDER[u]
                r = rows(k)
                if u == 0:
                    pe.wait_ge(pv_copied, 4 + NT)
                if u == KT:
                    pe.wait_ge(yT_ready, 1)
                pe.wait_ge(h_lo, u + 1)
                mm3(pvb[:, :], [wd_sb[0:r, s, k * D:(k + 1) * D] for s in range(2)],
                    [hs[0:r, u % 2, s, :] for s in range(2)], start=(u % KT == 0),
                    stop=(u % KT == KT - 1)).then_inc(down_done, 1)

            def transpose_y(hf):
                ps, full = claim(f"y_{hf}")
                pe.wait_ge(yT_ready, hf + 1)
                for n in range(TPH):
                    ins = nc.tensor.transpose(ps[:, n * P:(n + 1) * P], yT[:, n * P:(n + 1) * P], ident)
                ins.then_inc(full, 1)

            context_keys(0)
            transpose_xn(1, 0)
            context_keys(1)
            queries_keys(0)
            transpose_xn(1, 1)
            context_keys(2)
            scores(0)
            scores(1)
            queries_keys(1)
            scores(2)
            context_keys(3)
            values(0)
            context_values(0)
            context_values(1)
            scores(3)
            queries_keys(2)
            for i in range(NU):
                transpose_p(i)
                if i + 4 < NU and not 12 <= i <= 19:
                    scores(i + 4)
                if i == 2:
                    values(1)
                if i in (6, 9):
                    context_values(i // 3)
                if i == 4:
                    queries_keys(3)
                if i in (5, 8, 12):
                    attend((5, 8, 12).index(i))
                if i == 10:
                    project_o(0)
                if i == 12:
                    transpose_xn(2, 0)
                if i == 13:
                    context_keys(4)
                if i == 14:
                    cross_queries(0)
                if i == 15:
                    context_keys(5)
                    scores(16)
                    attend(3)
                    scores(17)
                    scores(18)
                    project_o(1)
                    context_keys(6)
                    scores(19)
                    context_keys(7)
                if i == 17:
                    transpose_xn(2, 1)
                if i - 1 >= NU1:
                    cross_attend(i - 1 - NU1)
                if i == 17:
                    context_values(4)
                    cross_queries(1)
                if i == 18:
                    scores(20)
                    scores(21)
                if i in (18, 19):
                    scores(i + 4)
                if i - 2 >= NU1:
                    cross_project(i - 2 - NU1)
                if 18 <= i <= 20:
                    context_values(i - 13)
            transpose_xn(3, 0)
            cross_attend(NT - 1)
            cross_project(NT - 2)
            gate(0)
            cross_project(NT - 1)
            for u in range(2 * KT):
                expert_up(u)
                if u == 1:
                    transpose_w(0)
                if u == 3:
                    transpose_xn(3, 1)
                if u == 5:
                    gate(1)
                if u == 11:
                    transpose_w(1)
                spread_w(u)
                if u >= 2:
                    expert_down(u - 2)
                if u == KT + 4:
                    transpose_y(0)
            expert_down(2 * KT - 2)
            expert_down(2 * KT - 1)
            transpose_y(1)


def _tables():
    f = np.float32
    row = np.arange(P)
    ident = np.eye(P, dtype=f)
    mask_h4 = (row[:, None] // D1 % HG == np.arange(HG)).astype(f)
    mask_h2 = (row[:, None] // S == np.arange(2)).astype(f)
    mask_g = (row[:, None] // (HG * D1) == np.arange(G)).astype(f)
    tri = np.broadcast_to((np.arange(E)[None, :] < np.arange(E)[:, None]).astype(f).reshape(1, E * E), (P, E * E))
    ones_h = np.concatenate([(np.arange(HG * D1)[None, :] // D1 == 2 * a + row[:, None] // S).astype(f)
                             for a in range(2)], axis=1)
    consts = np.concatenate([ident, mask_h4, mask_h2, mask_g, tri, ones_h], axis=1)
    inv_freq = (f(1.0) / f(10000.0) ** (np.arange(0, D1, 2, dtype=f) / f(D1))).astype(f)
    freqs = (np.arange(S, dtype=f)[None, :] * inv_freq[row % D1 % 4][:, None]).astype(f)
    sign = np.where(row % D1 < D1 // 2, -1.0, 1.0).astype(f)[:, None]
    rope = np.stack([np.cos(freqs), sign * np.sin(freqs)], axis=1).astype(f)
    selector = np.zeros((P, RT * P), np.float16)
    feature = np.arange(RT * P)
    selector[feature // F, feature] = 1
    selector[WLO + feature // F, feature] = 1
    return consts, rope, selector


def kernel(**inputs):
    import concourse.bacc as _bacc
    from concourse.bass_utils import run_bass_kernel_spmd as _run

    a = {k: np.asarray(v) for k, v in inputs.items()}
    heads = np.arange(D).reshape(H1, D1)
    straight = heads[:, [0, 2, 4, 6, 1, 3, 5, 7]].reshape(-1)
    swapped = heads[:, [1, 3, 5, 7, 0, 2, 4, 6]].reshape(-1)
    wq, wk, wv, wo = (a[f"L0_attn_W{n}"] for n in "qkvo")
    bq, bk, bv, bo = (a[f"L0_attn_b{n}"] for n in "qkvo")
    consts, rope, selector = _tables()
    arrays = {
        "x": a["x"].reshape(T, D),
        "ctxT": a["ctx_768"].reshape(T, DC).T,
        "attn_w": np.stack([wq[straight].T, wq[swapped].T, wk[straight].T, wk[swapped].T, wv.T, wo.T], axis=1),
        "attn_b": np.stack([bq[straight], bq[swapped], bk[straight], bk[swapped], bv], axis=1),
        "bias_rows": np.stack([bo, a["L0_xattn_bo"]]),
        "xw_q": a["L0_xattn_Wq"], "xw_k": a["L0_xattn_Wk"], "xw_v": a["L0_xattn_Wv"],
        "xw_o": a["L0_xattn_Wo"].reshape(2, 2, 2, D2, D).transpose(1, 3, 0, 2, 4).reshape(P, HP, D),
        "gate_w": a["L0_ffn_gate_w"],
        "w_gate": np.concatenate([a["L0_ffn_exp_gate"], a["L0_ffn_sh_gate"]]).transpose(1, 0, 2).reshape(D, FT),
        "w_up": np.concatenate([a["L0_ffn_exp_up"], a["L0_ffn_sh_up"]]).transpose(1, 0, 2).reshape(D, FT),
        "w_down": np.concatenate([a["L0_ffn_exp_down"], a["L0_ffn_sh_down"]]).reshape(FT, D),
        "consts": consts, "rope": rope, "selector": selector,
    }
    arrays = {f"{k}_dram": np.ascontiguousarray(v) for k, v in arrays.items()}
    nc = _bacc.Bacc("TRN2", target_bir_lowering=False, num_devices=1)
    args = [nc.dram_tensor(k, v.shape, mybir.dt.from_np(v.dtype), kind="ExternalInput").ap()
            for k, v in arrays.items()]
    out = nc.dram_tensor("out_dram", (T, D), mybir.dt.float32, kind="ExternalOutput").ap()
    decoder_layer(nc, *args, out)
    r = _run(nc, [arrays], core_ids=[0])
    return r.results[0]["out_dram"].reshape(B, S, D)
```

```python
from contextlib import ExitStack

import numpy as np
import concourse.bass as bass
from concourse import mybir

P = 128
B, S, D = 16, 64, 128
T = B * S
NT = T // P
HALF = T // 2
TPH = NT // 2
BPH = B // 2
H1, D1 = 16, 8
G, HG = 4, 4
H2, D2 = 8, 64
HP = H2 // 2
DC = 96
E, F, NSH = 8, 176, 2
FT = (E + NSH) * F
KT = -(-FT // P)
RT = E * F // P
assert RT * P == E * F
EPS = 1e-5
SCALE1, SCALE2 = D1 ** -0.5, D2 ** -0.5
NU1, NU = 16, 24
BLK = 8
WARM = 9
WLO = 32

ORDER = list(range(RT, KT)) + list(range(RT)) + list(range(RT)) + list(range(RT, KT))

MISC = (["ln1_0", "k_0", "q_0", "k_1", "q_1", "ln1_1", "v_0", "cv_0", "cv_1", "k_2", "q_2", "v_1",
         "k_3", "q_3", "cv_2", "cv_3", "wo_0", "ln2_0", "kx_4"]
        + [f"xq_0_{i}" for i in range(HP)] + ["kx_5", "kx_6", "wo_1", "kx_7", "cv_4", "ln2_1"]
        + [f"xq_1_{i}" for i in range(HP)] + ["cv_5", "xwo_0", "cv_6", "xwo_1", "cv_7", "xwo_2"]
        + [f"xwo_{p}" for p in range(3, 6)] + ["ln3_0", "xwo_6", "gate_0", "xwo_7"]
        + ["wt_0", "ln3_1", "gate_1", "wt_1"])
LN = ["ln1_0", "ln1_1", "ln2_0", "ln2_1", "ln3_0", "ln3_1"]


def decoder_layer(nc, x, ctxT, attn_w, attn_b, bias_rows, xw_q, xw_k, xw_v, xw_o, gate_w, w_gate, w_up,
                  w_down, consts, rope, selector, out):
    f32, f16 = mybir.dt.float32, mybir.dt.float16
    ALU, ACT, AX = mybir.AluOpType, mybir.ActivationFunctionType, mybir.AxisListType
    ctx = ExitStack()
    with ctx:
        def sb(name, shape, dt=f32):
            return ctx.enter_context(nc.sbuf_tensor(name, shape, dt))

        def sem(name):
            return ctx.enter_context(nc.semaphore(name))

        x_sb = sb("x_sb", [P, NT, D])
        xb_sb = sb("xb_sb", [P, NT, D])
        x2_sb = sb("x2_sb", [P, NT, D])
        x2b_sb = x_sb
        x3_sb = xb_sb
        xn_sb = sb("xn_sb", [P, 2, TPH, D])
        xnT = sb("xnT", [D, 2, T], f16)
        ctxT_sb = sb("ctxT_sb", [P, T])
        attn_w_sb = sb("attn_w_sb", [D, 2, 5, D], f16)
        wo_sb = sb("wo_sb", [D, D])
        attn_b_sb = sb("attn_b_sb", [D, 5])
        rows_sb = sb("rows_sb", [P, 2, D])
        xwq_sb = sb("xwq_sb", [D, 2, H2 * D2], f16)
        CH = H2 * D2
        xwk_sb = sb("xwk_sb", [P, CH])
        xwv_sb = sb("xwv_sb", [P, CH])
        stage = [sb(f"stage{i}", [P, CH]) for i in range(2)]
        xwo_sb = sb("xwo_sb", [P, HP, D])
        gate_raw = sb("gate_raw", [D, E])
        gate_sb = sb("gate_sb", [D, 2, E], f16)
        wg_sb = sb("wg_sb", [D, 2, FT], f16)
        wu_sb = sb("wu_sb", [D, 2, FT], f16)
        wd_sb = sb("wd_sb", [P, 2, KT * D], f16)
        consts_sb = sb("consts_sb", [P, D + HG + 2 + G + E * E + 2 * 32])
        ident = consts_sb[:, 0:D]
        mask_h4 = consts_sb[:, D:D + HG]
        mask_h2 = consts_sb[:, D + HG:D + HG + 2]
        mask_g = consts_sb[:, D + HG + 2:D + HG + 2 + G]
        tri = consts_sb[:, D + HG + 2 + G:D + HG + 2 + G + E * E]
        ones_h = consts_sb[:, D + HG + 2 + G + E * E:].rearrange("p (a c) -> p a c", a=2)
        rope_sb = sb("rope_sb", [D, 2, S])
        sel_sb = sb("sel_sb", [P, RT * P], f16)
        QT = 4 * S
        t12 = sb("t12", [D, 2 * HALF])
        OT = t12
        qkr = sb("qkr", [D, 2 * HALF])
        qr, kr = (qkr[:, :].rearrange("p (r k t) -> p r k t", r=2, k=2)[:, :, i, :] for i in range(2))
        qG = sb("qG", [D, G, T])
        kM = sb("kM", [D, B, HG, S])
        VM = sb("VM", [P, 2, NT, G, 2, 32])
        kxM = sb("kxM", [P, HP, B, 2, S])
        Vx = sb("Vx", [P, B, HP, D2])
        qx = qG
        mx = sb("mx", [P, 2, BLK])
        NE = 4
        sh = sb("sh", [P, 2, BLK * S])
        ex = sb("ex", [P, NE, BLK * S])
        ls = sb("ls", [P, NE, BLK])
        rs = sb("rs", [P, NE, BLK])
        rsum = sb("rsum", [P, QT])
        NPT = 6
        PT = sb("PT", [P, NPT, BLK * S])
        PTx = sb("PTx", [P, 2, BLK, 2, S])
        OTx = t12[:, 0:2 * HP * P].rearrange("p (r k s) -> p r k s", r=2, k=HP)
        st = sb("st", [P, TPH, 6])
        mv = sb("mv", [P, 2, TPH, 2])
        ve = sb("ve", [P, 2, TPH])
        rstd = sb("rstd", [P, 2, TPH])
        minus_half = sb("minus_half", [P, TPH])
        lg = sb("lg", [P, TPH, E])
        lm = sb("lm", [P, TPH])
        gt, eq = (qkr[:, i * TPH * E * E:(i + 1) * TPH * E * E].rearrange("p (n e f) -> p n e f", n=TPH, e=E)
                  for i in range(2))
        rank = sb("rank", [P, TPH, E])
        lsft = sb("lsft", [P, TPH, E])
        lex = sb("lex", [P, TPH, E])
        wk = sb("wk", [P, TPH, E])
        wsum = sb("wsum", [P, TPH])
        wrec = sb("wrec", [P, TPH])
        wte = sb("wte", [P, TPH, E])
        wT = sb("wT", [P, T], f16)
        ffn = qG[:, :, :].rearrange("p g t -> p (g t)").rearrange("p (n t) -> p n t", t=HALF)
        sg, hu, hh = ffn[:, 0:2, :], ffn[:, 2:4, :], ffn[:, 4:6, :]
        hs = ffn[:, 6:8, :].bitcast(f16).rearrange("p r (i t) -> p r i t", i=2)
        raw = qG[:, :, :].rearrange("p g t -> p (g t)")
        attn_raw, xwq_raw = raw[:, 0:5 * D], raw[:, 5 * D:5 * D + CH]
        y_sb = x2_sb

        bank = [ctx.enter_context(nc.psum_tensor(f"bank{i}", [P, 512], f32)) for i in range(8)]
        sbank = lambda u: bank[u % 3]
        tbank = lambda u: bank[3 + u % 2]
        kxbank = lambda i: bank[min(3 + i, 5)]
        pvb = bank[5]
        gbank = lambda u: bank[u % 2]
        ubank = lambda u: bank[2 + u % 2]
        wbank = bank[4]

        ld = {n: sem(f"ld_{n}") for n in ("x0", "x1", "ctx", "aw", "wo", "ab", "rows", "xq", "xk", "xv", "xo", "gw",
                                          "cst", "rope", "sel")}
        chunk_in = [sem(f"chunk_in{i}") for i in range(2)]
        chunk_hi = sem("chunk_hi")
        chunk_lo = sem("chunk_lo")
        aw_hi, aw_lo = sem("aw_hi"), sem("aw_lo")
        blank_ready = sem("blank_ready")
        padded = sem("padded")
        zeroed = sem("zeroed")
        dve_c = sem("dve_c")
        pool_c = sem("pool_c")
        misc_full = [sem(f"misc_full{i}") for i in range(2)]
        misc_free = [sem(f"misc_free{i}") for i in range(2)]
        gw_split = sem("gw_split")
        kx_full, kx_free = sem("kx_full"), sem("kx_free")
        xn_ready = sem("xn_ready")
        var_ready = sem("var_ready")
        rstd_ready = sem("rstd_ready")
        xnT_hi = sem("xnT_hi")
        k_rotated, q_rotated = sem("k_rotated"), sem("q_rotated")
        q0_masked = sem("q0_masked")
        q_masked = sem("q_masked")
        k_masked = sem("k_masked")
        s_full = sem("s_full")
        s_sub = sem("s_sub")
        e_ready = sem("e_ready")
        r_ready = sem("r_ready")
        p_ready = sem("p_ready")
        t_full = sem("t_full")
        t_copied = sem("t_copied")
        pv_full = sem("pv_full")
        pv_copied = sem("pv_copied")
        ot_ready = sem("ot_ready")
        xb_ready = sem("xb_ready")
        lsft_ready, lex_ready = sem("lsft_ready"), sem("lex_ready")
        wte_ready = sem("wte_ready")
        g_full, u_full, w_full = sem("g_full"), sem("u_full"), sem("w_full")
        sg_ready = sem("sg_ready")
        hu_ready = sem("hu_ready")
        h_ready = sem("h_ready")
        h_hi = sem("h_hi")
        h_lo = sem("h_lo")
        down_done = sem("down_done")
        y_ready = sem("y_ready")
        stored = sem("stored")

        def misc(name):
            i = MISC.index(name)
            return i % 2, i // 2

        def misc_claim(pe, name):
            b, n = misc(name)
            if n:
                pe.wait_ge(misc_free[b], n)
            return bank[6 + b], misc_full[b]

        def misc_read(eng, name):
            b, n = misc(name)
            eng.wait_ge(misc_full[b], n + 1)
            return bank[6 + b], misc_free[b]

        def routed_before(u):
            return sum(k < RT for k in ORDER[:u])

        def rows(k):
            return min(P, FT - k * P)

        CHUNKS = []
        for src, dst in ((w_gate, wg_sb), (w_up, wu_sb)):
            CHUNKS += [(src[:, c:min(c + CH, FT)], dst, D, slice(c, min(c + CH, FT))) for c in range(0, FT, CH)]
        for k in range(0, KT - 1, CH // D):
            n = min(CH // D, KT - 1 - k)
            CHUNKS.append((w_down[k * P:(k + n) * P].rearrange("(k p) d -> p k d", p=P), wd_sb, P,
                           slice(k * D, (k + n) * D)))
        CHUNK_AT = [3, 4, 7, 8, 10, 11, 12, 13, 16, 17, 18, 20, 21]
        assert len(CHUNK_AT) == len(CHUNKS) + 1
        last = FT - (KT - 1) * P
        CHUNKS.append((w_down[(KT - 1) * P:FT], wd_sb, last, slice((KT - 1) * D, KT * D)))

        def landed(eng, c):
            eng.wait_ge(chunk_in[c % 2], 16 * (c // 2 + 1))

        block = ctx.enter_context(nc.Block())

        @block.sync
        def _(sp):
            def load(name, dst, src):
                sp.dma_start(dst, src).then_inc(ld[name], 16)

            def load_x(hf):
                sp.dma_start(x_sb[:, hf * TPH:(hf + 1) * TPH, :],
                             x[hf * HALF:(hf + 1) * HALF].rearrange("(n p) d -> p n d", p=P)).then_inc(ld[f"x{hf}"], 16)

            load_x(0)
            load("xk", xwk_sb[0:DC, :], xw_k)
            load("aw", attn_raw, attn_w.rearrange("p k d -> p (k d)")[:, 0:5 * D])
            load_x(1)
            load("rope", rope_sb[:], rope)
            load("xv", xwv_sb[0:DC, :], xw_v)
            load("xq", xwq_raw, xw_q)
            load("rows", rows_sb[:], bias_rows.unsqueeze(0).broadcast_to([P, 2, D]))
            load("wo", wo_sb[:], attn_w[:, 5, :])
            load("xo", xwo_sb[:], xw_o)
            load("gw", gate_raw[:], gate_w)
            load("sel", sel_sb[:], selector)
            for c, (src, _, r, cols) in enumerate(CHUNKS):
                if c >= 2:
                    sp.wait_ge(chunk_lo, c - 1)
                dst = stage[c % 2][0:r, 0:cols.stop - cols.start]
                if len(src.shape) == 3:
                    dst = dst.rearrange("p (k d) -> p k d", d=D)
                sp.dma_start(dst, src).then_inc(chunk_in[c % 2], 16)
            for hf in range(2):
                sp.wait_ge(y_ready, hf + 1)
                sp.dma_start(out[hf * HALF:(hf + 1) * HALF].rearrange("(n p) d -> p n d", p=P),
                             y_sb[:, hf * TPH:(hf + 1) * TPH, :]).then_inc(stored, 16)
            sp.wait_ge(stored, 32)

        @block.gpsimd
        def _(pool):
            def rest(dst, src, k):
                pool.wait_ge(aw_hi, k)
                nc.gpsimd.tensor_tensor(dst[1], src, dst[0], ALU.subtract).then_inc(aw_lo, 1)

            def inverse_std(k):
                pool.wait_ge(var_ready, k + 1)
                if k >= 2:
                    pool.wait_ge(xn_ready, k - 1)
                nc.gpsimd.tensor_scalar(ve[:, k % 2, :], mv[:, k % 2, :, 1], EPS, None, ALU.add).then_inc(pool_c, 1)
                pool.wait_ge(pool_c, k + 2)
                nc.gpsimd.tensor_tensor(rstd[:, k % 2, :], ve[:, k % 2, :], minus_half[:],
                                        ALU.pow).then_inc(rstd_ready, 1)

            def mask_q(quad):
                pool.wait_ge(q_rotated, quad + 1)
                nc.gpsimd.tensor_tensor(qG[:, :, quad * QT:(quad + 1) * QT],
                                        qr[:, quad % 2, :].unsqueeze(1).broadcast_to([D, G, QT]),
                                        mask_g.unsqueeze(2).broadcast_to([D, G, QT]), ALU.mult).then_inc(q_masked, 1)

            def mask_k(quad):
                pool.wait_ge(k_rotated, quad + 1)
                nc.gpsimd.tensor_tensor(
                    kM[:, 4 * quad:4 * quad + 4],
                    kr[:, quad % 2, :].rearrange("p (b t) -> p b t", t=S).unsqueeze(2).broadcast_to([D, 4, HG, S]),
                    mask_h4.unsqueeze(1).unsqueeze(3).broadcast_to([D, 4, HG, S]), ALU.mult).then_inc(k_masked, 1)

            def split_chunk(c):
                _, dst, r, cols = CHUNKS[c]
                pool.wait_ge(chunk_hi, c + 1)
                nc.gpsimd.tensor_tensor(dst[0:r, 1, cols], stage[c % 2][0:r, 0:cols.stop - cols.start],
                                        dst[0:r, 0, cols], ALU.subtract).then_inc(chunk_lo, 1)

            def split_h(u):
                r = rows(ORDER[u])
                pool.wait_ge(h_hi, u + 1)
                nc.gpsimd.tensor_tensor(hs[0:r, u % 2, 1, :], hh[0:r, u % 2, :], hs[0:r, u % 2, 0, :],
                                        ALU.subtract).then_inc(h_lo, 1)

            def divide(u):
                pool.wait_ge(r_ready, u - NU1 + 1)
                v = ex[:, u % NE, :].rearrange("p (c t) -> p c t", t=S)
                nc.gpsimd.tensor_tensor(v, v, rs[:, u % NE, :].unsqueeze(2).broadcast_to([P, BLK, S]),
                                        ALU.mult).then_inc(p_ready, 1)

            def x2_bias(hf):
                b, n = misc(f"wo_{hf}")
                pool.wait_ge(misc_free[b], n + 1)
                tl = slice(hf * TPH, (hf + 1) * TPH)
                nc.gpsimd.tensor_tensor(x2b_sb[:, tl, :], x2_sb[:, tl, :],
                                        rows_sb[:, 1:2, :].broadcast_to([P, TPH, D]), ALU.add).then_inc(xb_ready, 1)

            nc.gpsimd.memset(sh[:, 0, :], 0.0).then_inc(blank_ready, 1)
            nc.gpsimd.memset(minus_half[:], -0.5).then_inc(pool_c, 1)
            pool.wait_ge(pool_c, 1)
            inverse_std(0)
            rest([attn_w_sb[:, i].rearrange("p k d -> p (k d)") for i in range(2)], attn_raw, 1)
            inverse_std(1)
            rest([xwq_sb[:, i] for i in range(2)], xwq_raw, 2)
            nc.gpsimd.memset(VM[:], 0.0).then_inc(zeroed, 1)
            nc.gpsimd.memset(wT[:], 0.0).then_inc(zeroed, 1)
            pool.wait_ge(ld["rows"], 16)
            pool.wait_ge(xn_ready, 2)
            nc.gpsimd.tensor_tensor(xb_sb[:], x_sb[:], rows_sb[:, 0:1, :].broadcast_to([P, NT, D]),
                                    ALU.add).then_inc(xb_ready, 1)
            nc.gpsimd.memset(PTx[:], 0.0).then_inc(zeroed, 1)
            mask_q(1)
            mask_q(2)
            mask_k(2)
            for c in range(3):
                split_chunk(c)
            mask_q(3)
            mask_k(3)
            for c in range(3, 8):
                split_chunk(c)
            inverse_std(2)
            split_chunk(8)
            x2_bias(0)
            for u in range(NU1, NU):
                divide(u)
                if u == 16:
                    inverse_std(3)
                if u == 17:
                    split_chunk(9)
                    split_chunk(10)
                if u == 19:
                    x2_bias(1)
                if u == 23:
                    inverse_std(4)
                if u in (20, 21):
                    split_chunk(u - 9)
            for u in range(2 * KT - 2):
                split_h(u)
                if u == 2:
                    inverse_std(5)

        @block.scalar
        def _(act):
            def copy_kx(i):
                hp, hf = i % HP, i // HP
                if hf == 0:
                    act.wait_ge(kx_full, i + 1)
                    ps, free = kxbank(i), kx_free
                else:
                    ps, free = misc_read(act, f"kx_{i}")
                if i == 0:
                    act.wait_ge(ld["cst"], 16)
                src = ps[:, :].rearrange("p (b t) -> p b t", t=S)
                for j in range(2):
                    ins = nc.scalar.activation(kxM[:, hp, hf * BPH:(hf + 1) * BPH, j, :], src, ACT.Copy,
                                               scale=mask_h2[:, j:j + 1])
                ins.then_inc(free, 1)

            def split_weights(dst, src, name):
                act.wait_ge(ld[name], 16)
                nc.scalar.copy(dst, src).then_inc(aw_hi, 1)

            def chunk_float16(c):
                _, dst, r, cols = CHUNKS[c]
                landed(act, c)
                nc.scalar.copy(dst[0:r, 0, cols], stage[c % 2][0:r, 0:cols.stop - cols.start]).then_inc(chunk_hi, 1)

            def copy_xnT(stage, hf):
                ps, _ = misc_read(act, f"ln{stage}_{hf}")
                nc.scalar.copy(xnT[:, 0, hf * HALF:(hf + 1) * HALF], ps[:, :]).then_inc(xnT_hi, 1)

            def copy_v(hf):
                if hf == 0:
                    act.wait_ge(zeroed, 1)
                ps, free = misc_read(act, f"v_{hf}")
                for b2 in range(2):
                    for h2 in range(2):
                        src = ps[b2 * S:(b2 + 1) * S, :].rearrange("p (n a h d) -> p n a h d",
                                                                   a=2, h=2, d=D1)[:, :, :, h2, :]
                        dst = VM[h2 * S:(h2 + 1) * S, b2, hf * TPH:(hf + 1) * TPH].rearrange(
                            "p n g a c -> p (n g) a c")
                        for a in range(2):
                            col = (2 * a + h2) * D1
                            ins = nc.scalar.copy(dst[:, :, a, col:col + D1], src[:, :, a, :])
                ins.then_inc(free, 1)

            def mask_k0():
                act.wait_ge(k_rotated, 1)
                for i in range(HG):
                    ins = nc.scalar.activation(kM[:, 0:4, i, :], kr[:, 0, :].rearrange("p (b t) -> p b t", t=S),
                                               ACT.Copy, scale=mask_h4[:, i:i + 1])
                ins.then_inc(k_masked, 1)

            def exponentials(u):
                act.wait_ge(s_sub, u + 1)
                if u >= NE:
                    act.wait_ge(t_full, u - NE + 1)
                nc.scalar.activation(ex[:, u % NE, :], sh[:, u % 2, :], ACT.Exp,
                                     scale=SCALE1 if u < NU1 else SCALE2).then_inc(e_ready, 1)

            def copy_t(u):
                act.wait_ge(t_full, u + 1)
                if u < NU1:
                    if u >= NPT:
                        act.wait_ge(pv_full, (u - NPT) // 4 + 1)
                    nc.scalar.copy(PT[:, u % NPT, :], tbank(u)[:, :]).then_inc(t_copied, 1)
                else:
                    if u == NU1:
                        act.wait_ge(zeroed, 3)
                    if u >= NU1 + 2:
                        act.wait_ge(pv_full, 4 + u - 2 - NU1 + 1)
                    src = tbank(u)[:, :].rearrange("p (c s) -> p c s", s=S)
                    for j in range(2):
                        r = slice(j * S, (j + 1) * S)
                        ins = nc.scalar.copy(PTx[r, u % 2, :, j, :], src[r])
                    ins.then_inc(t_copied, 1)

            def copy_cv(p):
                ps, free = misc_read(act, f"cv_{p}")
                for b2 in range(2):
                    for h2 in range(2):
                        src = ps[b2 * S:(b2 + 1) * S, :].rearrange("p (n h d) -> p n h d", h=2, d=D2)[:, :, h2, :]
                        ins = nc.scalar.copy(Vx[h2 * S:(h2 + 1) * S, 2 * p + b2, :, :], src)
                ins.then_inc(free, 1)

            def bias_ot(quad):
                act.wait_ge(pv_copied, quad + 1)
                o = OT[:, quad * QT:(quad + 1) * QT]
                nc.scalar.activation(o, o, ACT.Identity, bias=attn_b_sb[:, 4:5]).then_inc(ot_ready, 1)

            def copy_xq(hf):
                act.wait_ge(s_full, NU1 if hf else NU1 // 2)
                for hp in range(HP):
                    ps, free = misc_read(act, f"xq_{hf}_{hp}")
                    nc.scalar.copy(qx[:, hp, hf * HALF:(hf + 1) * HALF], ps[:, :]).then_inc(free, 1)

            def copy_otx(p):
                act.wait_ge(pv_full, 4 + p + 1)
                if p >= 2:
                    b, n = misc(f"xwo_{p - 2}")
                    act.wait_ge(misc_full[b], n + 1)
                nc.scalar.copy(OTx[:, p % 2, :, :].rearrange("p k s -> p (k s)"), pvb[:, :]).then_inc(pv_copied, 1)

            def router_exp(hf):
                act.wait_ge(lsft_ready, hf + 1)
                if hf:
                    act.wait_ge(wte_ready, hf)
                nc.scalar.activation(lex[:], lsft[:], ACT.Exp).then_inc(lex_ready, 1)

            def silu(u):
                r = rows(ORDER[u])
                act.wait_ge(g_full, u + 1)
                if u >= 2:
                    act.wait_ge(hu_ready, u - 1)
                nc.scalar.activation(sg[0:r, u % 2, :], gbank(u)[0:r, :], ACT.Silu).then_inc(sg_ready, 1)

            def h_float16(u):
                r = rows(ORDER[u])
                act.wait_ge(h_ready, u + 1)
                if u >= 2:
                    act.wait_ge(down_done, u - 1)
                nc.scalar.copy(hs[0:r, u % 2, 0, :], hh[0:r, u % 2, :]).then_inc(h_hi, 1)

            act.dma_start(ctxT_sb[0:DC, :], ctxT).then_inc(ld["ctx"], 16)
            act.dma_start(consts_sb[:], consts).then_inc(ld["cst"], 16)
            act.dma_start(attn_b_sb[:], attn_b).then_inc(ld["ab"], 16)
            split_weights(attn_w_sb[:, 0].rearrange("p k d -> p (k d)"), attn_raw, "aw")
            copy_xnT(1, 0)
            split_weights(xwq_sb[:, 0], xwq_raw, "xq")
            copy_kx(0)
            copy_kx(1)
            mask_k0()
            copy_kx(2)
            for j in range(NU + 4):
                if j == 16:
                    copy_t(14)
                    copy_t(15)
                if j == 18:
                    copy_kx(7)
                    copy_t(16)
                    copy_xnT(2, 1)
                    copy_cv(4)
                if j == 19:
                    copy_xq(1)
                    copy_t(17)
                    copy_otx(0)
                if j == 15:
                    copy_kx(4)
                if j == 17:
                    bias_ot(3)
                if j < NU:
                    exponentials(j)
                if j == 0:
                    copy_xnT(1, 1)
                    copy_v(0)
                if j in (1, 2):
                    copy_cv(j - 1)
                if j in (9, 12):
                    bias_ot(j // 3 - 3)
                if j == 16:
                    bias_ot(2)
                if 2 <= j < NU + 2 and not 16 <= j <= 19:
                    copy_t(j - 2)
                if j == 3:
                    copy_kx(3)
                if j == 4:
                    copy_v(1)
                if j in (9, 12):
                    copy_cv(j // 3 - 1)
                if j == 14:
                    copy_xnT(2, 0)
                if j == 15:
                    copy_xq(0)
                if j == 16:
                    copy_kx(5)
                if j == 17:
                    copy_kx(6)
                if NU1 < j - 3 < NU:
                    copy_otx(j - 3 - NU1)
                if j == 25:
                    copy_xnT(3, 0)
                if j == 19:
                    copy_cv(5)
                if j == 20:
                    copy_cv(6)
                if j == 21:
                    copy_cv(7)
                if j == 27:
                    router_exp(0)
                if j in CHUNK_AT:
                    chunk_float16(CHUNK_AT.index(j))
            for u in range(2 * KT + 1):
                if u < 2 * KT - 1:
                    silu(u)
                if u:
                    h_float16(u - 1)
                if u == 2 * KT - 1:
                    silu(u)
                if u == 5:
                    copy_xnT(3, 1)
                if u == 9:
                    router_exp(1)

        @block.vector
        def _(dve):
            chain = [0]

            def link(ins):
                chain[0] += 1
                ins.then_inc(dve_c, 1)
                dve.wait_ge(dve_c, chain[0])

            def statistics(k, src):
                hf = k % 2
                for n in range(TPH):
                    ins = nc.vector.bn_stats(st[:, n, :], src[:, hf * TPH + n, :])
                link(ins)
                for n in range(TPH):
                    ins = nc.vector.bn_aggr(mv[:, hf, n, :], st[:, n, :])
                ins.then_inc(var_ready, 1)
                dve.wait_ge(var_ready, k + 1)

            def normalise(k, src):
                hf = k % 2
                dve.wait_ge(rstd_ready, k + 1)
                if k >= 2:
                    b, n = misc(LN[k - 2])
                    dve.wait_ge(misc_full[b], n + 1)
                for n in range(TPH):
                    ins = nc.vector.tensor_scalar(xn_sb[:, hf, n, :], src[:, hf * TPH + n, :], mv[:, hf, n, 0:1],
                                                  rstd[:, hf, n:n + 1], ALU.subtract, ALU.mult)
                ins.then_inc(xn_ready, 1)

            def rest_xnT(k):
                tok = slice(k % 2 * HALF, (k % 2 + 1) * HALF)
                ps, free = misc_read(dve, LN[k])
                dve.wait_ge(xnT_hi, k + 1)
                nc.vector.tensor_tensor(xnT[:, 1, tok], ps[:, :], xnT[:, 0, tok], ALU.subtract).then_inc(free, 1)

            def rotate(quad):
                if quad == 0:
                    dve.wait_ge(ld["rope"], 16)
                    dve.wait_ge(ld["ab"], 16)
                for k, name, ready in ((1, "k", k_rotated), (0, "q", q_rotated)):
                    if quad:
                        dve.wait_ge(ready, quad)
                    ps, free = misc_read(dve, f"{name}_{quad}")
                    t = t12[:, k * HALF:(k + 1) * HALF].rearrange("p (i b s) -> p i b s", i=2, s=S)
                    for i in range(2):
                        ins = nc.vector.scalar_tensor_tensor(
                            t[:, i], ps[:, i * QT:(i + 1) * QT].rearrange("p (b s) -> p b s", s=S),
                            attn_b_sb[:, 2 * k + i:2 * k + i + 1],
                            rope_sb[:, i:i + 1, :].broadcast_to([D, 4, S]), ALU.add, ALU.mult)
                    ins.then_inc(free, 1)
                    b, n = misc(f"{name}_{quad}")
                    dve.wait_ge(misc_free[b], n + 1)
                    if k and quad == 2:
                        dve.wait_ge(k_masked, 1)
                    if not k and quad == 3:
                        dve.wait_ge(q_masked, 1)
                    dst = (kr if k else qr)[:, quad % 2, :].rearrange("p (b s) -> p b s", s=S)
                    nc.vector.tensor_tensor(dst, t[:, 0], t[:, 1], ALU.add).then_inc(ready, 1)

            def mask_q0():
                dve.wait_ge(q_rotated, 1)
                dve.wait_ge(aw_lo, 2)
                for g in range(G):
                    nc.vector.tensor_scalar(qG[:, g, 0:QT], qr[:, 0, :], mask_g[:, g:g + 1], None,
                                            ALU.mult).then_inc(q0_masked, 1)

            def mask_k1():
                dve.wait_ge(k_rotated, 2)
                for i in range(HG):
                    ins = nc.vector.tensor_scalar(kM[:, 4:8, i, :], kr[:, 1, :].rearrange("p (b t) -> p b t", t=S),
                                                  mask_h4[:, i:i + 1], None, ALU.mult)
                ins.then_inc(k_masked, 1)
                dve.wait_ge(k_masked, 2)

            def shift(u):
                dve.wait_ge(s_full, u + 1)
                v = sbank(u)[:, :].rearrange("p (c t) -> p c t", t=S)
                link(nc.vector.reduce_max(mx[:, u % 2, :], v, AX.X))
                if u >= 2:
                    dve.wait_ge(e_ready, u - 1)
                nc.vector.tensor_tensor(sh[:, u % 2, :].rearrange("p (c t) -> p c t", t=S), v,
                                        mx[:, u % 2, :].unsqueeze(2).broadcast_to([P, BLK, S]),
                                        ALU.subtract).then_inc(s_sub, 1)

            def sums(u):
                dve.wait_ge(e_ready, u + 1)
                if u >= NU1 + NE:
                    dve.wait_ge(p_ready, u - NU1 - NE + 1)
                link(nc.vector.reduce_sum(ls[:, u % NE, :], ex[:, u % NE, :].rearrange("p (c t) -> p c t", t=S), AX.X))
                nc.vector.reciprocal(rs[:, u % NE, :], ls[:, u % NE, :]).then_inc(r_ready, 1)

            def divide_ot(quad):
                dve.wait_ge(pv_full, quad + 1)
                link(nc.vector.reciprocal(rsum[:], pvb[:, QT:2 * QT]))
                if quad == 0:
                    dve.wait_ge(k_rotated, 4)
                    dve.wait_ge(q_rotated, 4)
                nc.vector.tensor_tensor(OT[:, quad * QT:(quad + 1) * QT], pvb[:, 0:QT], rsum[:],
                                        ALU.mult).then_inc(pv_copied, 1)
                dve.wait_ge(pv_copied, quad + 1)

            def add_x2(hf):
                dve.wait_ge(xb_ready, 1)
                ps, free = misc_read(dve, f"wo_{hf}")
                tl = slice(hf * TPH, (hf + 1) * TPH)
                nc.vector.tensor_tensor(x2_sb[:, tl, :].rearrange("p n d -> p (n d)"), ps[:, :],
                                        xb_sb[:, tl, :].rearrange("p n d -> p (n d)"), ALU.add).then_inc(free, 1)
                b, n = misc(f"wo_{hf}")
                dve.wait_ge(misc_free[b], n + 1)

            def add_x3(p):
                if p in (0, TPH):
                    dve.wait_ge(xb_ready, 2 + p // TPH)
                ps, free = misc_read(dve, f"xwo_{p}")
                nc.vector.tensor_tensor(x3_sb[:, p, :], ps[:, 0:D], x2b_sb[:, p, :], ALU.add).then_inc(free, 1)
                if p % TPH == TPH - 1:
                    b, n = misc(f"xwo_{p}")
                    dve.wait_ge(misc_free[b], n + 1)
                    b, n = misc(f"xwo_{p - 1}")
                    dve.wait_ge(misc_free[b], n + 1)

            def route_shift(hf):
                ps, free = misc_read(dve, f"gate_{hf}")
                link(nc.vector.tensor_copy(lg[:].rearrange("p n e -> p (n e)"), ps[:, 0:TPH * E]))
                nc.vector.reduce_max(lm[:], ps[:, 0:TPH * E].rearrange("p (n e) -> p n e", e=E), AX.X).then_inc(free, 1)
                b, n = misc(f"gate_{hf}")
                dve.wait_ge(misc_free[b], n + 1)
                if hf:
                    dve.wait_ge(lex_ready, hf)
                nc.vector.tensor_tensor(lsft[:], lg[:], lm[:].unsqueeze(2).broadcast_to([P, TPH, E]),
                                        ALU.subtract).then_inc(lsft_ready, 1)

            def route_compare():
                other = lg[:].unsqueeze(2).broadcast_to([P, TPH, E, E])
                own = lg[:].unsqueeze(3).broadcast_to([P, TPH, E, E])
                nc.vector.tensor_tensor(gt, other, own, ALU.is_gt)
                link(nc.vector.tensor_tensor(eq, other, own, ALU.is_equal))

            def route_rank():
                eqf = eq.rearrange("p n e f -> p n (e f)")
                link(nc.vector.tensor_tensor(eqf, eqf, tri.unsqueeze(1).broadcast_to([P, TPH, E * E]), ALU.mult))
                link(nc.vector.tensor_tensor(gt, gt, eq, ALU.add))
                link(nc.vector.reduce_sum(rank[:], gt, AX.X))

            def route_weights(hf):
                dve.wait_ge(lex_ready, hf + 1)
                link(nc.vector.scalar_tensor_tensor(wk[:], rank[:], 1.5, lex[:], ALU.is_lt, ALU.mult))
                link(nc.vector.reduce_sum(wsum[:], wk[:], AX.X))
                link(nc.vector.reciprocal(wrec[:], wsum[:]))
                if hf:
                    b, n = misc("wt_0")
                    dve.wait_ge(misc_full[b], n + 1)
                nc.vector.tensor_tensor(wte[:], wk[:], wrec[:].unsqueeze(2).broadcast_to([P, TPH, E]),
                                        ALU.mult).then_inc(wte_ready, 1)
                dve.wait_ge(wte_ready, hf + 1)

            def split_wT(hf):
                if hf == 0:
                    dve.wait_ge(zeroed, 2)
                ps, free = misc_read(dve, f"wt_{hf}")
                tok = slice(hf * HALF, (hf + 1) * HALF)
                link(nc.vector.tensor_copy(wT[0:E, tok], ps[0:E, :]))
                nc.vector.tensor_tensor(wT[WLO:WLO + E, tok], ps[0:E, :], wT[0:E, tok], ALU.subtract).then_inc(free, 1)
                b, n = misc(f"wt_{hf}")
                dve.wait_ge(misc_free[b], n + 1)

            def hidden(u):
                k = ORDER[u]
                r = rows(k)
                dve.wait_ge(sg_ready, u + 1)
                dve.wait_ge(u_full, u + 1)
                if u >= 2:
                    dve.wait_ge(h_lo, u - 1)
                routed = k < RT
                dst = hu[0:r, u % 2, :] if routed else hh[0:r, u % 2, :]
                nc.vector.tensor_tensor(dst, ubank(u)[0:r, :], sg[0:r, u % 2, :], ALU.mult).then_inc(hu_ready, 1)
                dve.wait_ge(hu_ready, u + 1)
                if routed:
                    dve.wait_ge(w_full, routed_before(u) + 1)
                    nc.vector.tensor_tensor(hh[:, u % 2, :], wbank[:, :], hu[:, u % 2, :], ALU.mult).then_inc(h_ready, 1)
                else:
                    dve.sem_inc(h_ready, 1)

            def rest_h(u):
                r = rows(ORDER[u])
                dve.wait_ge(h_hi, u + 1)
                dve.wait_ge(h_lo, u)
                nc.vector.tensor_tensor(hs[0:r, u % 2, 1, :], hh[0:r, u % 2, :], hs[0:r, u % 2, 0, :],
                                        ALU.subtract).then_inc(h_lo, 1)

            def add_y(hf):
                dve.wait_ge(down_done, KT * (hf + 1))
                tl = slice(hf * TPH, (hf + 1) * TPH)
                nc.vector.tensor_tensor(y_sb[:, tl, :].rearrange("p n d -> p (n d)"), pvb[:, :],
                                        x3_sb[:, tl, :].rearrange("p n d -> p (n d)"), ALU.add).then_inc(y_ready, 1)

            for t in (ctxT_sb, xwk_sb, xwv_sb):
                nc.vector.memset(t[DC:P, :], 0.0).then_inc(padded, 1)
            dve.wait_ge(ld["x0"], 16)
            statistics(0, x_sb)
            normalise(0, x_sb)
            dve.wait_ge(ld["x1"], 16)
            statistics(1, x_sb)
            rest_xnT(0)
            dve.wait_ge(ld["cst"], 16)
            rotate(0)
            mask_q0()
            normalise(1, x_sb)
            for j in range(NU + 4):
                if j < NU:
                    shift(j)
                if 0 <= j - 5 - NU1 < NT:
                    add_x3(j - 5 - NU1)
                if NU1 < j < NU and j not in (18, 20):
                    sums(j - 1)
                if j == NU - 1:
                    sums(j)
                if j == 17:
                    add_x2(1)
                    statistics(3, x2_sb)
                    sums(17)
                    normalise(3, x2_sb)
                if j == 0:
                    rotate(1)
                    rest_xnT(1)
                if j == 2:
                    mask_k1()
                if j == 3:
                    rotate(2)
                if j == 8:
                    rotate(3)
                if j == 10:
                    dve.wait_ge(ld["gw"], 16)
                    nc.vector.tensor_copy(gate_sb[:, 0, :], gate_raw[:]).then_inc(gw_split, 1)
                    dve.wait_ge(gw_split, 1)
                    nc.vector.tensor_tensor(gate_sb[:, 1, :], gate_raw[:], gate_sb[:, 0, :],
                                            ALU.subtract).then_inc(gw_split, 1)
                if j == 9:
                    divide_ot(0)
                if j == 12:
                    divide_ot(1)
                if j == 14:
                    add_x2(0)
                    statistics(2, x2_sb)
                if j == 15:
                    normalise(2, x2_sb)
                    rest_xnT(2)
                    divide_ot(2)
                if j == 16:
                    divide_ot(3)
                if j == 18:
                    rest_xnT(3)
                if j == 19:
                    sums(19)
                if j == 24:
                    statistics(4, x3_sb)
                if j == 25:
                    normalise(4, x3_sb)
                if j == 26:
                    rest_xnT(4)
                if j == 27:
                    route_shift(0)
                    route_compare()
                    route_rank()
                    route_weights(0)
            for u in range(2 * KT):
                if u == 2 * KT - 1:
                    rest_h(u - 1)
                hidden(u)
                if u == 0:
                    add_x3(NT - 1)
                if u == 1:
                    split_wT(0)
                if u == 2:
                    statistics(5, x3_sb)
                if u == 3:
                    normalise(5, x3_sb)
                if u == 5:
                    rest_xnT(5)
                if u == 7:
                    route_shift(1)
                if u == 8:
                    route_compare()
                if u == 9:
                    route_rank()
                if u == 10:
                    route_weights(1)
                if u == 12:
                    split_wT(1)
                if u == KT + 1:
                    add_y(0)
            rest_h(2 * KT - 1)
            add_y(1)

        @block.tensor
        def _(pe):
            mm = nc.tensor.matmul
            claimed = [0]

            def claim(name):
                assert MISC[claimed[0]] == name, (MISC[claimed[0]], name)
                claimed[0] += 1
                return misc_claim(pe, name)

            def mm3(ps, w, x, start=True, stop=True):
                mm(ps, w[0], x[0], start=start, stop=False)
                mm(ps, w[0], x[1], start=False, stop=False)
                return mm(ps, w[1], x[0], start=False, stop=stop)

            def tokens(a, b):
                return xnT[:, 0, a:b], xnT[:, 1, a:b]

            def context_keys(i):
                hp, hf = i % HP, i // HP
                if i == 0:
                    pe.wait_ge(ld["ctx"], 16)
                    pe.wait_ge(ld["xk"], 16)
                    pe.wait_ge(padded, 3)
                if hf == 0:
                    if i == 3:
                        pe.wait_ge(kx_free, 3)
                    ps, full = kxbank(i), kx_full
                else:
                    ps, full = claim(f"kx_{i}")
                mm(ps[:, :], xwk_sb[:, hp * P:(hp + 1) * P], ctxT_sb[:, hf * HALF:(hf + 1) * HALF],
                   start=True, stop=True).then_inc(full, 1)

            def transpose_xn(stage, hf):
                ps, full = claim(f"ln{stage}_{hf}")
                if stage == 1 and hf == 0:
                    pe.wait_ge(ld["cst"], 16)
                pe.wait_ge(xn_ready, 2 * (stage - 1) + hf + 1)
                for n in range(TPH):
                    ins = nc.tensor.transpose(ps[:, n * P:(n + 1) * P], xn_sb[:, hf, n, :], ident)
                ins.then_inc(full, 1)

            def xnT_wait(stage, hf):
                b, n = misc(f"ln{stage}_{hf}")
                pe.wait_ge(misc_free[b], n + 1)

            def queries_keys(quad):
                if quad == 0:
                    pe.wait_ge(aw_lo, 1)
                xnT_wait(1, quad // 2)
                for k, name in ((1, "k"), (0, "q")):
                    ps, full = claim(f"{name}_{quad}")
                    for i in range(2):
                        ins = mm3(ps[:, i * QT:(i + 1) * QT], [attn_w_sb[:, s, 2 * k + i, :] for s in range(2)],
                                  tokens(quad * QT, (quad + 1) * QT))
                    ins.then_inc(full, 1)

            def values(hf):
                xnT_wait(1, hf)
                ps, full = claim(f"v_{hf}")
                for n in range(TPH):
                    t = (hf * TPH + n) * P
                    ins = mm3(ps[:, n * P:(n + 1) * P], tokens(t, t + P), [attn_w_sb[:, s, 4, :] for s in range(2)])
                ins.then_inc(full, 1)

            def context_values(p):
                ps, full = claim(f"cv_{p}")
                if p == 0:
                    pe.wait_ge(ld["xv"], 16)
                mm(ps[:, :], ctxT_sb[:, p * P:(p + 1) * P], xwv_sb[:, :], start=True, stop=True).then_inc(full, 1)

            def scores(u):
                if u >= 3:
                    pe.wait_ge(s_sub, u - 2)
                if u < NU1:
                    quad, g = u // 4, u % 4
                    if quad == 0:
                        pe.wait_ge(q0_masked, g + 1)
                    else:
                        pe.wait_ge(q_masked, quad)
                    if g == 0:
                        pe.wait_ge(k_masked, quad + 1)
                    for pp in range(2):
                        for b2 in range(2):
                            b = 4 * quad + 2 * pp + b2
                            ins = mm(sbank(u)[b2 * S:(b2 + 1) * S, pp * HG * S:(pp + 1) * HG * S],
                                     qG[:, g, b * S:(b + 1) * S], kM[:, b].rearrange("p i t -> p (i t)"),
                                     start=True, stop=True)
                else:
                    p = u - NU1
                    if p % TPH == 0:
                        for hp in range(HP - 2, HP):
                            b, n = misc(f"xq_{p // TPH}_{hp}")
                            pe.wait_ge(misc_free[b], n + 1)
                    if p == TPH:
                        for i in (2 * HP - 2, 2 * HP - 1):
                            b, n = misc(f"kx_{i}")
                            pe.wait_ge(misc_free[b], n + 1)
                    for hp in range(HP):
                        for b2 in range(2):
                            b = 2 * p + b2
                            ins = mm(sbank(u)[b2 * S:(b2 + 1) * S, hp * P:(hp + 1) * P],
                                     qx[:, hp, b * S:(b + 1) * S], kxM[:, hp, b].rearrange("p j t -> p (j t)"),
                                     start=True, stop=True)
                ins.then_inc(s_full, 1)

            def transpose_p(u):
                if u < NU1:
                    pe.wait_ge(e_ready, u + 1)
                else:
                    pe.wait_ge(p_ready, u - NU1 + 1)
                if u < 2:
                    pe.wait_ge(kx_free, u + 1)
                if u >= 2:
                    pe.wait_ge(t_copied, u - 1)
                for c in range(4):
                    ins = nc.tensor.transpose(tbank(u)[:, c * P:(c + 1) * P], ex[:, u % NE, c * P:(c + 1) * P], ident)
                ins.then_inc(t_full, 1)

            def attend(quad):
                pe.wait_ge(t_copied, 4 * quad + 4)
                if quad % 2 == 0:
                    b, n = misc(f"v_{quad // 2}")
                    pe.wait_ge(misc_free[b], n + 1)
                if quad == 0:
                    pe.wait_ge(kx_free, HP)
                else:
                    pe.wait_ge(pv_copied, quad)
                for pp in range(2):
                    for b2 in range(2):
                        tile = 2 * quad + pp
                        col = (2 * pp + b2) * S
                        for a in range(2):
                            for g in range(G):
                                ptg = PT[:, (4 * quad + g) % NPT, :].rearrange("p (c s) -> p c s", s=S)
                                mm(pvb[32 * g:32 * (g + 1), col:col + S], VM[:, b2, tile, g, a, :],
                                   ptg[:, (2 * pp + a) * 2 + b2, :], start=(a == 0), stop=(a == 1),
                                   skip_group_check=True)
                for a in range(2):
                    for g in range(G):
                        ptg = PT[:, (4 * quad + g) % NPT, :].rearrange("p (q a t) -> p q a t", q=2, a=2)
                        ins = mm(pvb[32 * g:32 * (g + 1), QT:2 * QT].rearrange("p (q t) -> p q t", q=2),
                                 ones_h[:, a, :], ptg[:, :, a, :], start=(a == 0), stop=(a == 1),
                                 skip_group_check=True)
                ins.then_inc(pv_full, 1)

            def project_o(hf):
                ps, full = claim(f"wo_{hf}")
                pe.wait_ge(ot_ready, 2 * hf + 2)
                if hf == 0:
                    pe.wait_ge(ld["wo"], 16)
                for n in range(TPH):
                    t = (hf * TPH + n) * P
                    ins = mm(ps[:, n * P:(n + 1) * P], OT[:, t:t + P], wo_sb[:, :], start=True, stop=True)
                ins.then_inc(full, 1)

            def cross_queries(hf):
                if hf == 0:
                    pe.wait_ge(aw_lo, 2)
                xnT_wait(2, hf)
                for hp in range(HP):
                    ps, full = claim(f"xq_{hf}_{hp}")
                    mm3(ps[:, :], [xwq_sb[:, s, hp * P:(hp + 1) * P] for s in range(2)],
                        tokens(hf * HALF, (hf + 1) * HALF)).then_inc(full, 1)

            def cross_attend(p):
                u = NU1 + p
                pe.wait_ge(t_copied, u + 1)
                pe.wait_ge(pv_copied, 4 + p)
                b, n = misc(f"cv_{p}")
                pe.wait_ge(misc_free[b], n + 1)
                o = pvb[:, :].rearrange("p (j h b s) -> p j h b s", j=2, h=2, b=2)
                for j in range(2):
                    for b2 in range(2):
                        for c in range(2):
                            hp = 2 * j + c
                            ins = mm(o[c * S:(c + 1) * S, j, :, b2, :], Vx[:, 2 * p + b2, hp, :],
                                     PTx[:, u % 2, 2 * hp + b2, :, :], start=True, stop=True)
                ins.then_inc(pv_full, 1)

            def cross_project(p):
                if p == 0:
                    pe.wait_ge(ld["xo"], 16)
                ps, full = claim(f"xwo_{p}")
                pe.wait_ge(pv_copied, 4 + p + 1)
                for k in range(HP):
                    ins = mm(ps[:, 0:D], OTx[:, p % 2, k, :], xwo_sb[:, k, :], start=(k == 0), stop=(k == HP - 1))
                ins.then_inc(full, 1)

            def gate(hf):
                ps, full = claim(f"gate_{hf}")
                if hf == 0:
                    pe.wait_ge(gw_split, 2)
                xnT_wait(3, hf)
                for n in range(TPH):
                    t = (hf * TPH + n) * P
                    ins = mm3(ps[:, n * E:(n + 1) * E], tokens(t, t + P), [gate_sb[:, s, :] for s in range(2)])
                ins.then_inc(full, 1)

            def transpose_w(hf):
                ps, full = claim(f"wt_{hf}")
                pe.wait_ge(wte_ready, hf + 1)
                for n in range(TPH):
                    ins = nc.tensor.transpose(ps[0:E, n * P:(n + 1) * P], wte[:, n, :], ident)
                ins.then_inc(full, 1)

            def expert_up(u):
                hf, k = u // KT, ORDER[u]
                r = rows(k)
                x = tokens(hf * HALF, (hf + 1) * HALF)
                if u == 0:
                    pe.wait_ge(chunk_lo, len(CHUNKS))
                    pe.wait_ge(s_sub, NU)
                    pe.wait_ge(t_copied, NU)
                if u == KT:
                    xnT_wait(3, 1)
                if u >= 2:
                    pe.wait_ge(sg_ready, u - 1)
                mm3(gbank(u)[0:r, :], [wg_sb[:, s, k * P:k * P + r] for s in range(2)], x).then_inc(g_full, 1)
                if u >= 2:
                    pe.wait_ge(hu_ready, u - 1)
                mm3(ubank(u)[0:r, :], [wu_sb[:, s, k * P:k * P + r] for s in range(2)], x).then_inc(u_full, 1)

            def spread_w(u):
                hf, k = u // KT, ORDER[u]
                if k >= RT:
                    return
                if routed_before(u) == hf * RT:
                    b, n = misc(f"wt_{hf}")
                    pe.wait_ge(misc_free[b], n + 1)
                    if hf == 0:
                        pe.wait_ge(ld["sel"], 16)
                if routed_before(u):
                    pe.wait_ge(h_ready, u)
                mm(wbank[:, :], sel_sb[:, k * P:(k + 1) * P], wT[:, hf * HALF:(hf + 1) * HALF],
                   start=True, stop=True).then_inc(w_full, 1)

            def expert_down(u):
                hf, k = u // KT, ORDER[u]
                r = rows(k)
                if u == 0:
                    pe.wait_ge(pv_copied, 4 + NT)
                if u == KT:
                    pe.wait_ge(y_ready, 1)
                w = [wd_sb[0:r, s, k * D:(k + 1) * D] for s in range(2)]
                first, last = u % KT == 0, u % KT == KT - 1
                pe.wait_ge(h_hi, u + 1)
                for n in range(TPH):
                    for s in range(2):
                        mm(pvb[:, n * P:(n + 1) * P], hs[0:r, u % 2, 0, n * P:(n + 1) * P], w[s],
                           start=(first and n == 0 and s == 0), stop=False, skip_group_check=True)
                pe.wait_ge(h_lo, u + 1)
                for n in range(TPH):
                    ins = mm(pvb[:, n * P:(n + 1) * P], hs[0:r, u % 2, 1, n * P:(n + 1) * P], w[0],
                             start=False, stop=last, skip_group_check=True)
                ins.then_inc(down_done, 1)

            blank = sh[:, 0, :].bitcast(f16)
            pe.wait_ge(blank_ready, 1)
            for _ in range(WARM):
                mm(bank[7][:, :], blank[:, 0:P], blank[:, 512:1024], start=True, stop=True)
            context_keys(0)
            transpose_xn(1, 0)
            context_keys(1)
            queries_keys(0)
            context_keys(2)
            queries_keys(1)
            scores(0)
            scores(1)
            scores(2)
            context_keys(3)
            transpose_xn(1, 1)
            scores(3)
            values(0)
            transpose_p(0)
            context_values(0)
            context_values(1)
            for i in range(NU):
                if i == 17:
                    context_values(4)
                    transpose_xn(2, 1)
                if i:
                    transpose_p(i)
                if i == 0:
                    queries_keys(2)
                if i + 4 < NU and not 12 <= i <= 19:
                    scores(i + 4)
                if i == 2:
                    values(1)
                if i in (6, 9):
                    context_values(i // 3)
                if i == 4:
                    queries_keys(3)
                if i in (5, 8, 12):
                    attend((5, 8, 12).index(i))
                if i == 10:
                    project_o(0)
                if i == 12:
                    transpose_xn(2, 0)
                if i == 13:
                    context_keys(4)
                if i == 14:
                    cross_queries(0)
                if i == 15:
                    context_keys(5)
                    scores(16)
                    attend(3)
                    scores(17)
                    context_keys(6)
                    project_o(1)
                    scores(18)
                    scores(19)
                    context_keys(7)
                if i == 18:
                    scores(20)
                    scores(21)
                if i - 1 >= NU1:
                    cross_attend(i - 1 - NU1)
                if i == 17:
                    cross_queries(1)
                if i == 18:
                    context_values(5)
                if i in (18, 19):
                    scores(i + 4)
                if i - 2 >= NU1:
                    cross_project(i - 2 - NU1)
                if i in (18, 19):
                    context_values(i - 12)
            transpose_xn(3, 0)
            cross_project(NT - 2)
            cross_attend(NT - 1)
            gate(0)
            cross_project(NT - 1)
            for u in range(2 * KT):
                expert_up(u)
                if u == 1:
                    transpose_w(0)
                if u == 5:
                    transpose_xn(3, 1)
                if u == 7:
                    gate(1)
                if u == 12:
                    transpose_w(1)
                spread_w(u)
                if u >= 2:
                    expert_down(u - 2)
            expert_down(2 * KT - 2)
            expert_down(2 * KT - 1)


def _tables():
    f = np.float32
    row = np.arange(P)
    ident = np.eye(P, dtype=f)
    mask_h4 = (row[:, None] // D1 % HG == np.arange(HG)).astype(f)
    mask_h2 = (row[:, None] // S == np.arange(2)).astype(f)
    mask_g = (row[:, None] // (HG * D1) == np.arange(G)).astype(f)
    tri = np.broadcast_to((np.arange(E)[None, :] < np.arange(E)[:, None]).astype(f).reshape(1, E * E), (P, E * E))
    ones_h = np.concatenate([(np.arange(HG * D1)[None, :] // D1 == 2 * a + row[:, None] // S).astype(f)
                             for a in range(2)], axis=1)
    consts = np.concatenate([ident, mask_h4, mask_h2, mask_g, tri, ones_h], axis=1)
    inv_freq = (f(1.0) / f(10000.0) ** (np.arange(0, D1, 2, dtype=f) / f(D1))).astype(f)
    freqs = (np.arange(S, dtype=f)[None, :] * inv_freq[row % D1 % 4][:, None]).astype(f)
    sign = np.where(row % D1 < D1 // 2, -1.0, 1.0).astype(f)[:, None]
    rope = np.stack([np.cos(freqs), sign * np.sin(freqs)], axis=1).astype(f)
    selector = np.zeros((P, RT * P), np.float16)
    feature = np.arange(RT * P)
    selector[feature // F, feature] = 1
    selector[WLO + feature // F, feature] = 1
    return consts, rope, selector


def kernel(**inputs):
    import concourse.bacc as _bacc
    from concourse.bass_utils import run_bass_kernel_spmd as _run

    a = {k: np.asarray(v) for k, v in inputs.items()}
    heads = np.arange(D).reshape(H1, D1)
    straight = heads[:, [0, 2, 4, 6, 1, 3, 5, 7]].reshape(-1)
    swapped = heads[:, [1, 3, 5, 7, 0, 2, 4, 6]].reshape(-1)
    wq, wk, wv, wo = (a[f"L0_attn_W{n}"] for n in "qkvo")
    bq, bk, bv, bo = (a[f"L0_attn_b{n}"] for n in "qkvo")
    consts, rope, selector = _tables()
    arrays = {
        "x": a["x"].reshape(T, D),
        "ctxT": a["ctx_768"].reshape(T, DC).T,
        "attn_w": np.stack([wq[straight].T, wq[swapped].T, wk[straight].T, wk[swapped].T, wv.T, wo.T], axis=1),
        "attn_b": np.stack([bq[straight], bq[swapped], bk[straight], bk[swapped], bv], axis=1),
        "bias_rows": np.stack([bo, a["L0_xattn_bo"]]),
        "xw_q": a["L0_xattn_Wq"], "xw_k": a["L0_xattn_Wk"], "xw_v": a["L0_xattn_Wv"],
        "xw_o": a["L0_xattn_Wo"].reshape(2, 2, 2, D2, D).transpose(1, 3, 0, 2, 4).reshape(P, HP, D),
        "gate_w": a["L0_ffn_gate_w"],
        "w_gate": np.concatenate([a["L0_ffn_exp_gate"], a["L0_ffn_sh_gate"]]).transpose(1, 0, 2).reshape(D, FT),
        "w_up": np.concatenate([a["L0_ffn_exp_up"], a["L0_ffn_sh_up"]]).transpose(1, 0, 2).reshape(D, FT),
        "w_down": np.concatenate([a["L0_ffn_exp_down"], a["L0_ffn_sh_down"]]).reshape(FT, D),
        "consts": consts, "rope": rope, "selector": selector,
    }
    arrays = {f"{k}_dram": np.ascontiguousarray(v) for k, v in arrays.items()}
    nc = _bacc.Bacc("TRN2", target_bir_lowering=False, num_devices=1)
    args = [nc.dram_tensor(k, v.shape, mybir.dt.from_np(v.dtype), kind="ExternalInput").ap()
            for k, v in arrays.items()]
    out = nc.dram_tensor("out_dram", (T, D), mybir.dt.float32, kind="ExternalOutput").ap()
    decoder_layer(nc, *args, out)
    r = _run(nc, [arrays], core_ids=[0])
    return r.results[0]["out_dram"].reshape(B, S, D)
```
